# Optimizing a Trainium2 kernel written in Bass

```python
import numpy as np
import jax
import jax.numpy as jnp

def _softmax(x, axis=-1):
    return jax.nn.softmax(x, axis=axis)

def _gelu(x):
    return jax.nn.gelu(x, approximate=True)

def _silu(x):
    return jax.nn.silu(x)

def _sigmoid(x):
    return jax.nn.sigmoid(x)

def _layernorm(x, axis=-1, eps=1e-05):
    m = jnp.mean(x, axis=axis, keepdims=True)
    v = jnp.var(x, axis=axis, keepdims=True)
    return (x - m) / jnp.sqrt(v + eps)

def _scatter_add(tgt, idx, src, axis=0):
    return tgt.at[idx].add(src)

def _segment_sum(src, seg, n):
    return jax.ops.segment_sum(src, seg, n)
kernel_name = 'mk_flamingo_gated_d4_seqx_r8_082fab'

def setup_inputs(seed: int=0):
    np.random.seed(seed)
    _w = jnp.asarray

    def _rec_inputs():
        import jax
        import jax.numpy as jnp
        _rk = jax.random.key(seed)
        x = -7.109e-05 + 0.9999 * jax.random.normal(jax.random.fold_in(_rk, 1), (8, 256, 128), jnp.float32)
        _lenS = 256 - jax.random.randint(jax.random.fold_in(_rk, 7), (8,), 0, max(1, 256 // 4) + 1, jnp.int32)
        _lenS2 = 256 - jax.random.randint(jax.random.fold_in(_rk, 8), (8,), 0, max(1, 256 // 4) + 1, jnp.int32)
        _ctx_768P = jax.random.normal(jax.random.fold_in(_rk, 11), (8, 16, 96), jnp.float32)
        _ctx_768c = jax.random.dirichlet(jax.random.fold_in(_rk, 511), 0.3 * jnp.ones((16,), jnp.float32), (8, 256))
        _ctx_768t = jnp.einsum('bsk,bkd->bsd', _ctx_768c, _ctx_768P)
        _ctx_768t = _ctx_768t * jax.lax.rsqrt(jnp.mean(jnp.square(_ctx_768t)) + 1e-12) * 0.953939
        ctx_768 = 0.000486113 + 1.00014 * (_ctx_768t + 0.3 * jax.random.normal(jax.random.fold_in(_rk, 611), (8, 256, 96), jnp.float32))
        _g = jax.random.normal(jax.random.fold_in(_rk, 9001), (2, 4), jnp.float32)
        _g = jnp.sign(_g) * jnp.maximum(jnp.abs(_g), 1.0) + (_g == 0) * 1.0
        g_xattn = _g[0]
        g_ffn = _g[1]
        return (x, ctx_768, g_xattn, g_ffn)
    x, ctx_768, g_xattn, g_ffn = _rec_inputs()

    def _L0_xattn_setup():
        import jax, jax.numpy as jnp
        import numpy as np
        import math
        B, L, E = (16, 512, 128)
        LC, EC = (77, 96)
        H = 16
        DH = E // H
        key = jax.random.key(seed)
        ks = jax.random.split(key, 10)
        s = 0.02
        return {'x': jax.random.normal(ks[0], (B, L, E), jnp.float32), 'cross': jax.random.normal(ks[1], (B, LC, EC), jnp.float32), 'q_w': jax.random.normal(ks[2], (E, E), jnp.float32) * s, 'q_b': jax.random.normal(ks[3], (E,), jnp.float32) * s, 'k_w': jax.random.normal(ks[4], (E, EC), jnp.float32) * s, 'k_b': jax.random.normal(ks[5], (E,), jnp.float32) * s, 'v_w': jax.random.normal(ks[6], (E, EC), jnp.float32) * s, 'v_b': jax.random.normal(ks[7], (E,), jnp.float32) * s, 'o_w': jax.random.normal(ks[8], (E, E), jnp.float32) * s, 'o_b': jax.random.normal(ks[9], (E,), jnp.float32) * s}
    _L0_xattn_all = _L0_xattn_setup()
    _L0_xattn_in = {k: v for k, v in _L0_xattn_all.items() if k in ('q_w', 'q_b', 'k_w', 'k_b', 'v_w', 'v_b', 'o_w', 'o_b')}
    del _L0_xattn_all

    def _L0_ffn_setup():
        import jax, jax.numpy as jnp
        import numpy as np
        QMAX = 127.0

        def _ste_round(v):
            return v + jax.lax.stop_gradient(jnp.round(v) - v)

        def _act_fake_quant(x, clip_factor):
            scale = jax.nn.sigmoid(clip_factor) * jnp.max(jnp.abs(x)) / QMAX
            return jnp.clip(_ste_round(x / scale), -QMAX - 1.0, QMAX) * scale

        def _weight_fake_quant(w):
            scale = jnp.max(jnp.abs(w), axis=1, keepdims=True) / QMAX
            return jnp.clip(_ste_round(w / scale), -QMAX - 1.0, QMAX) * scale
        key = jax.random.key(seed)
        k1, k2, k3, k4 = jax.random.split(key, 4)
        B, S, H, I = (8, 1024, 128, 352)
        return {'x': jax.random.normal(k1, (B, S, H), dtype=jnp.float32), 'clip_x': jnp.full((1,), 4.0, dtype=jnp.float32), 'clip_down': jnp.full((1,), 4.0, dtype=jnp.float32), 'w_gate': jax.random.normal(k2, (I, H), dtype=jnp.float32) * 0.02, 'w_up': jax.random.normal(k3, (I, H), dtype=jnp.float32) * 0.02, 'w_down': jax.random.normal(k4, (H, I), dtype=jnp.float32) * 0.02}
    _L0_ffn_all = _L0_ffn_setup()
    _L0_ffn_in = {k: v for k, v in _L0_ffn_all.items() if k in ('clip_x', 'clip_down', 'w_gate', 'w_up', 'w_down')}
    del _L0_ffn_all

    def _L1_xattn_setup():
        import jax, jax.numpy as jnp
        import numpy as np
        HEADS = 16
        DIM_HEAD = 64
        key = jax.random.key(seed)
        ks = jax.random.split(key, 7)
        B, Nq, Dq = (4, 256, 128)
        Nk, Dc = (128, 96)
        inner = HEADS * DIM_HEAD
        sq = 1.0 / np.sqrt(Dq)
        sc = 1.0 / np.sqrt(Dc)
        si = 1.0 / np.sqrt(inner)
        return {'x': jax.random.normal(ks[0], (B, Nq, Dq), dtype=jnp.float32), 'context': jax.random.normal(ks[1], (B, Nk, Dc), dtype=jnp.float32), 'Wq': jax.random.normal(ks[2], (Dq, inner), dtype=jnp.float32) * sq, 'Wk': jax.random.normal(ks[3], (Dc, inner), dtype=jnp.float32) * sc, 'Wv': jax.random.normal(ks[4], (Dc, inner), dtype=jnp.float32) * sc, 'Wo': jax.random.normal(ks[5], (inner, Dq), dtype=jnp.float32) * si, 'bo': jax.random.normal(ks[6], (Dq,), dtype=jnp.float32) * 0.01}
    _L1_xattn_all = _L1_xattn_setup()
    _L1_xattn_in = {k: v for k, v in _L1_xattn_all.items() if k in ('Wq', 'Wk', 'Wv', 'Wo', 'bo')}
    del _L1_xattn_all

    def _L1_ffn_setup():
        import jax, jax.numpy as jnp
        import numpy as np
        B, S, DIM, FFN, E = (4, 256, 128, 512, 8)
        key = jax.random.key(seed)
        k0, k1, k2, k3 = jax.random.split(key, 4)
        scale = 0.02
        return {'hidden_states': jax.random.normal(k0, (B, S, DIM), jnp.float32), 'router_w': jax.random.normal(k1, (DIM, E), jnp.float32) * scale, 'router_b': jnp.zeros((E,), jnp.float32), 'w1': jax.random.normal(k2, (E, DIM, 2 * FFN), jnp.float32) * scale, 'w2': jax.random.normal(k3, (E, FFN, DIM), jnp.float32) * scale}
    _L1_ffn_all = _L1_ffn_setup()
    _L1_ffn_in = {k: v for k, v in _L1_ffn_all.items() if k in ('router_w', 'router_b', 'w1', 'w2')}
    del _L1_ffn_all

    def _L2_xattn_setup():
        import jax, jax.numpy as jnp
        import numpy as np
        HEADS = 8
        DIM_HEAD = 128
        ATTN_MATRIX_SCALE = 1.5
        SCALE = DIM_HEAD ** (-0.5)

        def _split_heads(t):
            b, n, _ = t.shape
            t = t.reshape(b, n, HEADS, DIM_HEAD)
            return t.transpose(2, 0, 1, 3).reshape(HEADS, b * n, DIM_HEAD)
        key = jax.random.key(seed)
        ks = jax.random.split(key, 7)
        b, n, m = (2, 256, 256)
        qd, cd, inner = (128, 96, HEADS * DIM_HEAD)
        x = jax.random.normal(ks[0], (b, n, qd), dtype=jnp.float32)
        context = jax.random.normal(ks[1], (b, m, cd), dtype=jnp.float32)
        Wq = jax.random.normal(ks[2], (qd, inner), dtype=jnp.float32) * qd ** (-0.5)
        Wk = jax.random.normal(ks[3], (cd, inner), dtype=jnp.float32) * cd ** (-0.5)
        Wv = jax.random.normal(ks[4], (cd, inner), dtype=jnp.float32) * cd ** (-0.5)
        Wout = jax.random.normal(ks[5], (inner, qd), dtype=jnp.float32) * inner ** (-0.5)
        bout = jnp.zeros((qd,), dtype=jnp.float32)
        return {'x': x, 'context': context, 'Wq': Wq, 'Wk': Wk, 'Wv': Wv, 'Wout': Wout, 'bout': bout}
    _L2_xattn_all = _L2_xattn_setup()
    _L2_xattn_in = {k: v for k, v in _L2_xattn_all.items() if k in ('Wq', 'Wk', 'Wv', 'Wout', 'bout')}
    del _L2_xattn_all

    def _L2_ffn_setup():
        import jax, jax.numpy as jnp
        import numpy as np
        B, T, D = (2, 256, 128)
        E, K, FF = (8, 2, 512)

        def _reference_tuple_inner(x, gate_w, gate_b, w1, b1, w2, b2):
            n_experts = w1.shape[0]
            gate_logits = x @ gate_w + gate_b
            topk_vals, topk_idx = jax.lax.top_k(gate_logits, K)
            topk_w = jax.nn.softmax(topk_vals, axis=-1)
            onehot = jax.nn.one_hot(topk_idx, n_experts, dtype=x.dtype)
            comb = jnp.sum(onehot * topk_w[..., None], axis=2)
            h = jax.nn.gelu(jnp.einsum('btd,edf->ebtf', x, w1) + b1[:, None, None, :], approximate=False)
            y = jnp.einsum('ebtf,efd->ebtd', h, w2) + b2[:, None, None, :]
            output = jnp.einsum('ebtd,bte->btd', y, comb)
            expert_counts = jnp.sum(onehot, axis=(0, 1, 2)).astype(jnp.float32)
            return (output, gate_logits, topk_idx, expert_counts)
        key = jax.random.key(seed)
        ks = jax.random.split(key, 4)
        scale = 0.02
        return {'x': jax.random.normal(ks[0], (B, T, D), jnp.float32), 'gate_w': jax.random.normal(ks[1], (D, E), jnp.float32) * scale, 'gate_b': jnp.zeros((E,), jnp.float32), 'w1': jax.random.normal(ks[2], (E, D, FF), jnp.float32) * scale, 'b1': jnp.zeros((E, FF), jnp.float32), 'w2': jax.random.normal(ks[3], (E, FF, D), jnp.float32) * scale, 'b2': jnp.zeros((E, D), jnp.float32)}
    _L2_ffn_all = _L2_ffn_setup()
    _L2_ffn_in = {k: v for k, v in _L2_ffn_all.items() if k in ('gate_w', 'gate_b', 'w1', 'b1', 'w2', 'b2')}
    del _L2_ffn_all

    def _L3_xattn_setup():
        import jax, jax.numpy as jnp
        import numpy as np
        NUM_HEADS = 16
        HEAD_DIM = 64
        INNER = NUM_HEADS * HEAD_DIM
        QUERY_DIM = 128
        CONTEXT_DIM = 96
        SCALE = HEAD_DIM ** (-0.5)
        key = jax.random.key(seed)
        ks = jax.random.split(key, 6)
        B, NQ, NKV = (8, 128, 256)
        query = jax.random.normal(ks[0], (B, NQ, QUERY_DIM), dtype=jnp.float32)
        context = jax.random.normal(ks[1], (B, NKV, CONTEXT_DIM), dtype=jnp.float32)
        w_q = jax.random.normal(ks[2], (QUERY_DIM, INNER), dtype=jnp.float32) * QUERY_DIM ** (-0.5)
        w_kv = jax.random.normal(ks[3], (CONTEXT_DIM, 2 * INNER), dtype=jnp.float32) * CONTEXT_DIM ** (-0.5)
        w_out = jax.random.normal(ks[4], (INNER, QUERY_DIM), dtype=jnp.float32) * INNER ** (-0.5)
        b_out = jax.random.normal(ks[5], (QUERY_DIM,), dtype=jnp.float32) * 0.01
        return {'query': query, 'context': context, 'w_q': w_q, 'w_kv': w_kv, 'w_out': w_out, 'b_out': b_out}
    _L3_xattn_all = _L3_xattn_setup()
    _L3_xattn_in = {k: v for k, v in _L3_xattn_all.items() if k in ('w_q', 'w_kv', 'w_out', 'b_out')}
    del _L3_xattn_all

    def _L3_ffn_setup():
        import jax, jax.numpy as jnp
        import numpy as np
        B, S, H = (2, 256, 128)
        E, K, F_EXP, F_SHARED = (16, 2, 64, 128)
        key = jax.random.key(seed)
        ks = jax.random.split(key, 9)
        sc = 1.0 / np.sqrt(H)
        scf = 1.0 / np.sqrt(F_EXP)
        scfs = 1.0 / np.sqrt(F_SHARED)
        return {'x': jax.random.normal(ks[0], (B, S, H), dtype=jnp.float32), 'router_w': jax.random.normal(ks[1], (H, E), dtype=jnp.float32) * sc, 'gate_w': jax.random.normal(ks[2], (E, H, F_EXP), dtype=jnp.float32) * sc, 'up_w': jax.random.normal(ks[3], (E, H, F_EXP), dtype=jnp.float32) * sc, 'down_w': jax.random.normal(ks[4], (E, F_EXP, H), dtype=jnp.float32) * scf, 'shared_gate_w': jax.random.normal(ks[5], (H, F_SHARED), dtype=jnp.float32) * sc, 'shared_up_w': jax.random.normal(ks[6], (H, F_SHARED), dtype=jnp.float32) * sc, 'shared_down_w': jax.random.normal(ks[7], (F_SHARED, H), dtype=jnp.float32) * scfs}
    _L3_ffn_all = _L3_ffn_setup()
    _L3_ffn_in = {k: v for k, v in _L3_ffn_all.items() if k in ('router_w', 'gate_w', 'up_w', 'down_w', 'shared_gate_w', 'shared_up_w', 'shared_down_w')}
    del _L3_ffn_all
    return {'x': x, 'ctx_768': ctx_768, 'g_xattn': g_xattn, 'g_ffn': g_ffn, 'L0_xattn_q_w': _L0_xattn_in['q_w'], 'L0_xattn_q_b': _L0_xattn_in['q_b'], 'L0_xattn_k_w': _L0_xattn_in['k_w'], 'L0_xattn_k_b': _L0_xattn_in['k_b'], 'L0_xattn_v_w': _L0_xattn_in['v_w'], 'L0_xattn_v_b': _L0_xattn_in['v_b'], 'L0_xattn_o_w': _L0_xattn_in['o_w'], 'L0_xattn_o_b': _L0_xattn_in['o_b'], 'L0_ffn_clip_x': _L0_ffn_in['clip_x'], 'L0_ffn_clip_down': _L0_ffn_in['clip_down'], 'L0_ffn_w_gate': _L0_ffn_in['w_gate'], 'L0_ffn_w_up': _L0_ffn_in['w_up'], 'L0_ffn_w_down': _L0_ffn_in['w_down'], 'L1_xattn_Wq': _L1_xattn_in['Wq'], 'L1_xattn_Wk': _L1_xattn_in['Wk'], 'L1_xattn_Wv': _L1_xattn_in['Wv'], 'L1_xattn_Wo': _L1_xattn_in['Wo'], 'L1_xattn_bo': _L1_xattn_in['bo'], 'L1_ffn_router_w': _L1_ffn_in['router_w'], 'L1_ffn_router_b': _L1_ffn_in['router_b'], 'L1_ffn_w1': _L1_ffn_in['w1'], 'L1_ffn_w2': _L1_ffn_in['w2'], 'L2_xattn_Wq': _L2_xattn_in['Wq'], 'L2_xattn_Wk': _L2_xattn_in['Wk'], 'L2_xattn_Wv': _L2_xattn_in['Wv'], 'L2_xattn_Wout': _L2_xattn_in['Wout'], 'L2_xattn_bout': _L2_xattn_in['bout'], 'L2_ffn_gate_w': _L2_ffn_in['gate_w'], 'L2_ffn_gate_b': _L2_ffn_in['gate_b'], 'L2_ffn_w1': _L2_ffn_in['w1'], 'L2_ffn_b1': _L2_ffn_in['b1'], 'L2_ffn_w2': _L2_ffn_in['w2'], 'L2_ffn_b2': _L2_ffn_in['b2'], 'L3_xattn_w_q': _L3_xattn_in['w_q'], 'L3_xattn_w_kv': _L3_xattn_in['w_kv'], 'L3_xattn_w_out': _L3_xattn_in['w_out'], 'L3_xattn_b_out': _L3_xattn_in['b_out'], 'L3_ffn_router_w': _L3_ffn_in['router_w'], 'L3_ffn_gate_w': _L3_ffn_in['gate_w'], 'L3_ffn_up_w': _L3_ffn_in['up_w'], 'L3_ffn_down_w': _L3_ffn_in['down_w'], 'L3_ffn_shared_gate_w': _L3_ffn_in['shared_gate_w'], 'L3_ffn_shared_up_w': _L3_ffn_in['shared_up_w'], 'L3_ffn_shared_down_w': _L3_ffn_in['shared_down_w']}

def reference(x, ctx_768, g_xattn, g_ffn, L0_xattn_q_w, L0_xattn_q_b, L0_xattn_k_w, L0_xattn_k_b, L0_xattn_v_w, L0_xattn_v_b, L0_xattn_o_w, L0_xattn_o_b, L0_ffn_clip_x, L0_ffn_clip_down, L0_ffn_w_gate, L0_ffn_w_up, L0_ffn_w_down, L1_xattn_Wq, L1_xattn_Wk, L1_xattn_Wv, L1_xattn_Wo, L1_xattn_bo, L1_ffn_router_w, L1_ffn_router_b, L1_ffn_w1, L1_ffn_w2, L2_xattn_Wq, L2_xattn_Wk, L2_xattn_Wv, L2_xattn_Wout, L2_xattn_bout, L2_ffn_gate_w, L2_ffn_gate_b, L2_ffn_w1, L2_ffn_b1, L2_ffn_w2, L2_ffn_b2, L3_xattn_w_q, L3_xattn_w_kv, L3_xattn_w_out, L3_xattn_b_out, L3_ffn_router_w, L3_ffn_gate_w, L3_ffn_up_w, L3_ffn_down_w, L3_ffn_shared_gate_w, L3_ffn_shared_up_w, L3_ffn_shared_down_w):
    import jax
    import jax.numpy as jnp

    def _L0_xattn_ref(x, cross, q_w, q_b, k_w, k_b, v_w, v_b, o_w, o_b):
        import jax, jax.numpy as jnp
        import numpy as np
        import math
        B, L, E = (16, 512, 128)
        LC, EC = (77, 96)
        H = 16
        DH = E // H
        b, l, e = x.shape
        q = jnp.einsum('ble,fe->blf', x, q_w) + q_b
        k = jnp.einsum('bce,fe->bcf', cross, k_w) + k_b
        v = jnp.einsum('bce,fe->bcf', cross, v_w) + v_b
        q = q.reshape(b, l, H, DH).transpose(0, 2, 1, 3)
        v = v.reshape(b, -1, H, DH).transpose(0, 2, 1, 3)
        scores = jnp.einsum('bhld,bhcd->bhlc', q, v) / math.sqrt(DH)
        attn = jax.nn.softmax(scores, axis=-1)
        qkv = jnp.einsum('bhlc,bhcd->bhld', attn, v)
        qkv = qkv.reshape(b, l, e)
        out = jnp.einsum('ble,fe->blf', qkv, o_w) + o_b
        return out

    def _L0_ffn_ref(x, clip_x, clip_down, w_gate, w_up, w_down):
        import jax, jax.numpy as jnp
        import numpy as np
        QMAX = 127.0

        def _ste_round(v):
            return v + jax.lax.stop_gradient(jnp.round(v) - v)

        def _act_fake_quant(x, clip_factor):
            scale = jax.nn.sigmoid(clip_factor) * jnp.max(jnp.abs(x)) / QMAX
            return jnp.clip(_ste_round(x / scale), -QMAX - 1.0, QMAX) * scale

        def _weight_fake_quant(w):
            scale = jnp.max(jnp.abs(w), axis=1, keepdims=True) / QMAX
            return jnp.clip(_ste_round(w / scale), -QMAX - 1.0, QMAX) * scale
        xq = _act_fake_quant(x, clip_x[0])
        gate = jnp.einsum('bsh,ih->bsi', xq, _weight_fake_quant(w_gate))
        up = jnp.einsum('bsh,ih->bsi', xq, _weight_fake_quant(w_up))
        h = _act_fake_quant(jax.nn.silu(gate) * up, clip_down[0])
        return jnp.einsum('bsi,hi->bsh', h, _weight_fake_quant(w_down))

    def _L1_xattn_ref(x, context, Wq, Wk, Wv, Wo, bo):
        import jax, jax.numpy as jnp
        import numpy as np
        HEADS = 16
        DIM_HEAD = 64
        B, Nq, _ = x.shape
        Nk = context.shape[1]
        h, dh = (HEADS, DIM_HEAD)
        q = (x @ Wq).reshape(B, Nq, h, dh)
        k = (context @ Wk).reshape(B, Nk, h, dh)
        v = (context @ Wv).reshape(B, Nk, h, dh)
        scale = 1.0 / jnp.sqrt(jnp.asarray(dh, dtype=x.dtype))
        scores = jnp.einsum('bqhd,bkhd->bhqk', q, k) * scale
        attn = jax.nn.softmax(scores, axis=-1)
        out = jnp.einsum('bhqk,bkhd->bqhd', attn, v).reshape(B, Nq, h * dh)
        return out @ Wo + bo

    def _L1_ffn_ref(hidden_states, router_w, router_b, w1, w2):
        import jax, jax.numpy as jnp
        import numpy as np
        B, S, DIM, FFN, E = (4, 256, 128, 512, 8)
        b, s, d = hidden_states.shape
        x = hidden_states.reshape(-1, d)
        logits = x @ router_w + router_b
        route = jax.nn.softmax(logits, axis=1)
        max_prob = jnp.max(route, axis=1, keepdims=True)
        max_ind = jnp.argmax(route, axis=1)
        out = jnp.zeros_like(x)
        num_experts = w1.shape[0]
        for e in range(num_experts):
            h = x @ w1[e]
            a, g = jnp.split(h, 2, axis=1)
            y = jax.nn.silu(a) * g @ w2[e]
            out = jnp.where((max_ind == e)[:, None], y, out)
        out = out * max_prob
        return out.reshape(b, s, d)

    def _L2_xattn_ref(x, context, Wq, Wk, Wv, Wout, bout):
        import jax, jax.numpy as jnp
        import numpy as np
        HEADS = 8
        DIM_HEAD = 128
        ATTN_MATRIX_SCALE = 1.5
        SCALE = DIM_HEAD ** (-0.5)

        def _split_heads(t):
            b, n, _ = t.shape
            t = t.reshape(b, n, HEADS, DIM_HEAD)
            return t.transpose(2, 0, 1, 3).reshape(HEADS, b * n, DIM_HEAD)
        b, n, _ = x.shape
        qh = _split_heads(jnp.einsum('bnq,qi->bni', x, Wq))
        kh = _split_heads(jnp.einsum('bmc,ci->bmi', context, Wk))
        vh = _split_heads(jnp.einsum('bmc,ci->bmi', context, Wv))
        sim = jnp.einsum('hid,hjd->hij', qh, kh) * SCALE
        mean = jnp.mean(sim, axis=-1, keepdims=True)
        sim = (sim - mean) * ATTN_MATRIX_SCALE + mean
        attn = jax.nn.softmax(sim, axis=-1)
        out = jnp.einsum('hij,hjd->hid', attn, vh)
        out = out.reshape(HEADS, b, n, DIM_HEAD).transpose(1, 2, 0, 3)
        out = out.reshape(b, n, HEADS * DIM_HEAD)
        return jnp.einsum('bni,iq->bnq', out, Wout) + bout

    def _L2_ffn_ref(x, gate_w, gate_b, w1, b1, w2, b2):
        import jax, jax.numpy as jnp
        import numpy as np
        B, T, D = (2, 256, 128)
        E, K, FF = (8, 2, 512)

        def _reference_tuple_inner(x, gate_w, gate_b, w1, b1, w2, b2):
            n_experts = w1.shape[0]
            gate_logits = x @ gate_w + gate_b
            topk_vals, topk_idx = jax.lax.top_k(gate_logits, K)
            topk_w = jax.nn.softmax(topk_vals, axis=-1)
            onehot = jax.nn.one_hot(topk_idx, n_experts, dtype=x.dtype)
            comb = jnp.sum(onehot * topk_w[..., None], axis=2)
            h = jax.nn.gelu(jnp.einsum('btd,edf->ebtf', x, w1) + b1[:, None, None, :], approximate=False)
            y = jnp.einsum('ebtf,efd->ebtd', h, w2) + b2[:, None, None, :]
            output = jnp.einsum('ebtd,bte->btd', y, comb)
            expert_counts = jnp.sum(onehot, axis=(0, 1, 2)).astype(jnp.float32)
            return (output, gate_logits, topk_idx, expert_counts)
        return _reference_tuple_inner(x, gate_w, gate_b, w1, b1, w2, b2)[0]

    def _L3_xattn_ref(query, context, w_q, w_kv, w_out, b_out):
        import jax, jax.numpy as jnp
        import numpy as np
        NUM_HEADS = 16
        HEAD_DIM = 64
        INNER = NUM_HEADS * HEAD_DIM
        QUERY_DIM = 128
        CONTEXT_DIM = 96
        SCALE = HEAD_DIM ** (-0.5)
        B, NQ, _ = query.shape
        NKV = context.shape[1]
        q = query @ w_q
        kv = context @ w_kv
        k, v = jnp.split(kv, 2, axis=-1)
        q = q.reshape(B, NQ, NUM_HEADS, HEAD_DIM).transpose(0, 2, 1, 3)
        k = k.reshape(B, NKV, NUM_HEADS, HEAD_DIM).transpose(0, 2, 1, 3)
        v = v.reshape(B, NKV, NUM_HEADS, HEAD_DIM).transpose(0, 2, 1, 3)
        scores = jnp.einsum('bhqd,bhkd->bhqk', q, k) * SCALE
        attn = jax.nn.softmax(scores, axis=-1)
        out = jnp.einsum('bhqk,bhkd->bhqd', attn, v)
        out = out.transpose(0, 2, 1, 3).reshape(B, NQ, INNER)
        return out @ w_out + b_out

    def _L3_ffn_ref(x, router_w, gate_w, up_w, down_w, shared_gate_w, shared_up_w, shared_down_w):
        import jax, jax.numpy as jnp
        import numpy as np
        B, S, H = (2, 256, 128)
        E, K, F_EXP, F_SHARED = (16, 2, 64, 128)
        b, s, h = x.shape
        T = b * s
        x_flat = x.reshape(T, h)
        shared_out = jax.nn.silu(x @ shared_gate_w) * (x @ shared_up_w) @ shared_down_w
        router_probs = jax.nn.softmax(x_flat @ router_w, axis=-1)
        topk_probs, topk_idx = jax.lax.top_k(router_probs, K)
        coeff = jnp.einsum('tk,tke->te', topk_probs, jax.nn.one_hot(topk_idx, E, dtype=x.dtype))

        def expert_step(acc, ws):
            g, u, d, c = ws
            inter = jax.nn.silu(x_flat @ g) * (x_flat @ u)
            return (acc + inter @ d * c[:, None], None)
        routed, _ = jax.lax.scan(expert_step, jnp.zeros((T, h), dtype=x.dtype), (gate_w, up_w, down_w, coeff.T))
        return routed.reshape(b, s, h) + shared_out
    x = x + jnp.tanh(g_xattn[0]) * _L0_xattn_ref(_layernorm(x, axis=-1), ctx_768, L0_xattn_q_w, L0_xattn_q_b, L0_xattn_k_w, L0_xattn_k_b, L0_xattn_v_w, L0_xattn_v_b, L0_xattn_o_w, L0_xattn_o_b)
    x = x + jnp.tanh(g_ffn[0]) * _L0_ffn_ref(_layernorm(x, axis=-1), L0_ffn_clip_x, L0_ffn_clip_down, L0_ffn_w_gate, L0_ffn_w_up, L0_ffn_w_down)
    x = x + jnp.tanh(g_xattn[1]) * _L1_xattn_ref(_layernorm(x, axis=-1), ctx_768, L1_xattn_Wq, L1_xattn_Wk, L1_xattn_Wv, L1_xattn_Wo, L1_xattn_bo)
    x = x + jnp.tanh(g_ffn[1]) * _L1_ffn_ref(_layernorm(x, axis=-1), L1_ffn_router_w, L1_ffn_router_b, L1_ffn_w1, L1_ffn_w2)
    x = x + jnp.tanh(g_xattn[2]) * _L2_xattn_ref(_layernorm(x, axis=-1), ctx_768, L2_xattn_Wq, L2_xattn_Wk, L2_xattn_Wv, L2_xattn_Wout, L2_xattn_bout)
    x = x + jnp.tanh(g_ffn[2]) * _L2_ffn_ref(_layernorm(x, axis=-1), L2_ffn_gate_w, L2_ffn_gate_b, L2_ffn_w1, L2_ffn_b1, L2_ffn_w2, L2_ffn_b2)
    x = x + jnp.tanh(g_xattn[3]) * _L3_xattn_ref(_layernorm(x, axis=-1), ctx_768, L3_xattn_w_q, L3_xattn_w_kv, L3_xattn_w_out, L3_xattn_b_out)
    x = x + jnp.tanh(g_ffn[3]) * _L3_ffn_ref(_layernorm(x, axis=-1), L3_ffn_router_w, L3_ffn_gate_w, L3_ffn_up_w, L3_ffn_down_w, L3_ffn_shared_gate_w, L3_ffn_shared_up_w, L3_ffn_shared_down_w)
    return x

_drawn_inputs = setup_inputs


def setup_inputs(seed=0):
    import zlib

    import numpy as np

    out = dict(_drawn_inputs(seed))
    spreads = {'L1_ffn_router_b': (0.0, 0.8),
     'L2_xattn_bout': (0.0, 0.596),
     'L2_ffn_gate_b': (0.0, 0.385),
     'L2_ffn_b1': (0.0, 2.0),
     'L2_ffn_b2': (0.0, 0.554)}
    factors = {'g_ffn': 27.92,
     'L0_xattn_q_w': 8.0,
     'L0_xattn_q_b': 8.0,
     'L0_xattn_v_w': 2.97,
     'L0_xattn_v_b': 8.0,
     'L0_xattn_o_w': 2.959,
     'L0_xattn_o_b': 2.985,
     'L0_ffn_w_gate': 5.71,
     'L0_ffn_w_up': 5.429,
     'L0_ffn_w_down': 5.573,
     'L1_xattn_bo': 4.678,
     'L1_ffn_router_w': 8.0,
     'L1_ffn_w1': 8.0,
     'L1_ffn_w2': 8.0,
     'L3_xattn_b_out': 32.348,
     'L2_ffn_gate_w': 2.673,
     'L2_ffn_w1': 6.576}
    for name, (base, spread) in spreads.items():
        noise = np.random.default_rng([zlib.crc32(name.encode()), seed]).standard_normal(out[name].shape)
        drawn = base * np.exp(spread * noise) if base else spread * noise
        out[name] = jnp.asarray(drawn.astype(out[name].dtype))
    for name, factor in factors.items():
        out[name] = (out[name] * factor).astype(out[name].dtype)
    return out
```

```python
from collections import namedtuple
from contextlib import ExitStack

import concourse.bass as bass
import numpy as np
from concourse import mybir

F32 = mybir.dt.float32
F16 = mybir.dt.float16
BF16 = mybir.dt.bfloat16
ALU = mybir.AluOpType
ACT = mybir.ActivationFunctionType
AX = mybir.AxisListType
RMAX = bass.bass_isa.ReduceOp.max

P = 128
D = 128
DC = 96
DA = DC + 1
NTOK = 2048
NT = NTOK // P
QB = 512
NQ = NTOK // QB
TQ = QB // P
SEQ = 256
QS = 64.0
EPS = 1e-5
ROUND = 12582912.0
QMAX = 127.0
Layer = namedtuple("Layer", "H DH scale wide CW")
LAYERS = (
    Layer(16, 8, 8 ** -0.5, False, 8),
    Layer(16, 64, 64 ** -0.5, False, D),
    Layer(8, 128, 1.5 * 128 ** -0.5, True, D),
    Layer(16, 64, 64 ** -0.5, False, D),
)
INTER = 352
IC = (128, 128, 96)


def build(nc, d, out):
    with ExitStack() as ctx:
        M = persistent(nc, ctx)
        prepare(nc, M, d)
        for n in range(4):
            layernorm(nc, M, 2 * n, split=True, plain=False, bias=n)
            attention(nc, M, n)
            if n == 0:
                gathered_projection(nc, M)
            layernorm(nc, M, 2 * n + 1, split=n > 0, plain=True, bias=None)
            if n == 0:
                quantised_ffn(nc, M)
            else:
                router(nc, M, d, n)
                expert_ffn(nc, M, d, n)
        store(nc, M, out)


class Memory:
    pass


def persistent(nc, ctx):
    M = Memory()

    def sb(name, shape, dt):
        return ctx.enter_context(nc.sbuf_tensor(name, shape, dt))

    M.x = sb("x_res", [P, NT, D], F32)
    M.xn = sb("x_norm", [P, NT, D], F32)
    M.xt = sb("x_normT", [P, NTOK], F32)
    M.xt_hi = sb("x_normT_hi", [P, NTOK], F16)
    M.xt_lo = sb("x_normT_lo", [P, NTOK], F16)
    M.ct_hi = sb("ctxT_hi", [DA, NTOK], F16)
    M.ct_lo = sb("ctxT_lo", [DC, NTOK], F16)
    M.cv_hi = sb("ctx_hi", [P, NT, P], F16)
    M.cv_lo = sb("ctx_lo", [P, NT, P], F16)
    M.A_hi = [sb(f"A{n}_hi", [P, L.H, DC], F16) for n, L in enumerate(LAYERS)]
    M.A_lo = [sb(f"A{n}_lo", [P, L.H, DC], F16) for n, L in enumerate(LAYERS)]
    M.C = [sb(f"C{n}", [DA, L.H + 1, L.CW + 1], F32) for n, L in enumerate(LAYERS)]
    M.vbias = sb("v_bias", [P, 17, 8], F32)
    M.wo0 = sb("wo0", [P, D], F32)
    M.o_dram = nc.dram_tensor("o_scratch", [17, NTOK, 8], F32, kind="Internal").ap()
    M.qbias = sb("q_bias", [DC, LAYERS[0].H], F32)
    M.obias = sb("out_bias", [P, 4, D], F32)
    M.gate = sb("gates", [P, 8], F32)
    M.ident = sb("ident", [P, P], F32)
    M.ident16 = sb("ident16", [P, P], F16)
    M.neghalf = sb("neg_half", [P, NT], F32)
    M.one = sb("one", [P, 1], F32)
    M.U = sb("u_out", [DA, 2, QB], F32)
    M.wgq = sb("w_gate_q", [P, INTER], BF16)
    M.wuq = sb("w_up_q", [P, INTER], BF16)
    M.wgs = sb("w_gate_s", [P, 3], F32)
    M.wus = sb("w_up_s", [P, 3], F32)
    M.wdT = sb("w_downT", [P, 3, D], F32)
    M.clip = sb("clips", [P, 2], F32)
    M.comb = sb("comb", [P, NT, 18], F32)
    M.ps = ctx.enter_context(nc.psum_tensor("ps", [P, 8, 512], F32))
    M.splits = 0
    M.sem_ln = {k: nc.alloc_semaphore(f"ln_{k}") for k in
                ("stat", "var", "rstd", "norm", "transposed", "hi")}
    return M


def prepare(nc, M, d):
    with ExitStack() as ctx:
        def sb(name, shape, dt):
            return ctx.enter_context(nc.sbuf_tensor(name, shape, dt))

        raw = [sb(f"raw{i}", [P, 16 * (2 * D + 2 * DC)], F32) for i in range(2)]
        cT = sb("ctxT_raw", [DC, NTOK], F32)
        cV = sb("ctx_raw", [P, NT, DC], F32)
        bq = sb("bq", [8, 16], F32)
        wv0 = sb("wv0", [DC, 16, 8], F32)
        bo = sb("bo", [1, 4, D], F32)
        ones = sb("ones_row", [1, P], F32)
        wn = sb("w_nat", [P, 6, D], F32)
        wd = sb("w_down", [P, INTER], F32)
        wr = sb("w_rounded", [P, 6, D], F32)
        wdr = sb("w_down_rounded", [P, INTER], F32)
        wi = sb("w_int", [P, 6, D], F32)
        am = sb("w_absmax", [P, 8], F32)
        sc = sb("w_scale", [P, 8], F32)
        inv = sb("w_inv", [P, 8], F32)

        loaded = {k: nc.alloc_semaphore(f"loaded_{k}") for k in ("x", "ctx", "small", "w0", "w1", "w2", "w3", "ffn")}
        zeroed = nc.alloc_semaphore("prep_zeroed")
        tanh_done = nc.alloc_semaphore("prep_tanh")
        split_done = nc.alloc_semaphore("prep_ctx_split")
        prod = nc.alloc_semaphore("prep_products")
        a_hi = nc.alloc_semaphore("prep_a_hi")
        evac = nc.alloc_semaphore("prep_evacuated")
        chain = nc.alloc_semaphore("prep_chain")
        wq_ready = nc.alloc_semaphore("prep_quantised")

        def views(n):
            L = LAYERS[n]
            r, at, v = raw[n % 2], 0, []
            for w in (D, DC, DC, D):
                v.append(r[0:L.DH, at:at + L.H * w].rearrange("p (h w) -> p h w", h=L.H))
                at += L.H * w
            return v

        names = (("L0_q", "L0_k"), ("L1_q", "L1_k", "L1_v", "L1_o"),
                 ("L2_q", "L2_k", "L2_v", "L2_o"), ("L3_q", "L3_k", "L3_v", "L3_o"))
        groups = [(n, h, kind) for n, L in enumerate(LAYERS) for h in range(0, L.H, 4) for kind in ("AC" if n else "A")]
        after = [sum(1 for g in groups if g[0] <= n) for n in range(4)]

        with nc.Block() as block:
            @block.sync
            def _(sp):
                for n in range(4):
                    if n >= 2:
                        sp.wait_ge(prod, after[n - 2])
                    for v, name in zip(views(n), names[n]):
                        sp.dma_start(v, d[name]).then_inc(loaded[f"w{n}"], 16)
                    if n == 0:
                        sp.dma_start(M.x[:], d["x"].rearrange("(t p) f -> p t f", p=P)).then_inc(loaded["x"], 16)
                sp.wait_ge(loaded["x"], 16)

            @block.scalar
            def _(act):
                for dst, name in ((bq[:], "L0_bq"), (wv0[:], "L0_wv"), (bo[:], "bo"), (M.gate[:], "g"),
                                  (M.clip[:], "clip"), (M.wo0[:], "L0_wo"), (M.vbias[:, 1:17, :], "L0_bv")):
                    act.dma_start(dst, d[name]).then_inc(loaded["small"], 16)
                act.dma_start(cT[:], d["ctxT"]).then_inc(loaded["ctx"], 16)
                act.dma_start(cV[:], d["ctx"].rearrange("(t p) f -> p t f", p=P)).then_inc(loaded["ctx"], 16)
                for j, name in enumerate(("L0_gate", "L0_up")):
                    act.dma_start(wn[:, 3 * j:3 * j + 2, :], d[name][0:2 * P, :].rearrange("(c p) f -> p c f", p=P)
                                  ).then_inc(loaded["ffn"], 16)
                    act.dma_start(wn[0:IC[2], 3 * j + 2, :], d[name][2 * P:INTER, :]).then_inc(loaded["ffn"], 16)
                act.dma_start(wd[:], d["L0_down"]).then_inc(loaded["ffn"], 16)
                act.wait_ge(loaded["small"], 7 * 16)
                nc.scalar.activation(M.gate[:], M.gate[:], ACT.Tanh).then_inc(tanh_done, 1)
                act.wait_ge(loaded["ctx"], 32)
                act.wait_ge(zeroed, 6)
                nc.scalar.activation(M.ct_hi[0:DC, :], cT[:], ACT.Copy).then_inc(split_done, 1)
                nc.scalar.activation(M.cv_hi[:, :, 0:DC], cV[:], ACT.Copy).then_inc(split_done, 1)
                na = 0
                for g, (n, h, kind) in enumerate(groups):
                    if kind == "A":
                        act.wait_ge(prod, g + 1)
                        na += 1
                        nc.scalar.activation(
                            M.A_hi[n][:, h:h + 4, :], M.ps[:, g % 6, 0:4 * DC].rearrange("p (h w) -> p h w", h=4),
                            ACT.Copy, scale=QS * LAYERS[n].scale).then_inc(a_hi, 1)

            @block.gpsimd
            def _(pool):
                link = chained(pool, zeroed)

                def fill(ap, value=0.0):
                    link(nc.gpsimd.memset(ap, value))

                fill(M.ident[:])
                link(nc.gpsimd.affine_select(out=M.ident[:], in_=M.ident[:], compare_op=ALU.not_equal, fill=1.0,
                                             base=0, pattern=[[-1, P]], channel_multiplier=1))
                fill(M.cv_hi[:])
                fill(M.cv_lo[:])
                fill(M.ct_hi[DC:DA, :], 1.0)
                fill(M.cv_hi[:, :, DC:DA], 1.0)
                fill(ones[:], 1.0)
                fill(am[:])
                fill(M.neghalf[:], -0.5)
                fill(M.one[:], 1.0)
                fill(M.U[:, 1, :])
                for n in range(4):
                    fill(M.C[n][:])
                link(nc.gpsimd.tensor_copy(M.ident16[:], M.ident[:]))
                fill(M.U[DC:DA, 1, :], 1.0)
                for n, L in enumerate(LAYERS):
                    fill(M.C[n][DC:DA, :, L.CW:L.CW + 1], 1.0)
                fill(M.vbias[:, 0, :])

            ALL_ZEROED = 22

            @block.tensor
            def _(pe):
                for g, (n, h0, kind) in enumerate(groups):
                    if g == 0 or groups[g - 1][0] != n:
                        pe.wait_ge(loaded[f"w{n}"], 16 * len(names[n]))
                    if g >= 6:
                        pe.wait_ge(evac, g - 5)
                    wq, wk, wv, wo = views(n)
                    wv = wk if n == 0 else wv
                    for j in range(4):
                        h = h0 + j
                        if kind == "A":
                            last = nc.tensor.matmul(M.ps[:, g % 6, j * DC:(j + 1) * DC], wq[:, h, :], wk[:, h, :],
                                                    start=True, stop=True)
                        else:
                            last = nc.tensor.matmul(M.ps[0:DC, g % 6, j * D:(j + 1) * D], wv[:, h, :], wo[:, h, :],
                                                    start=True, stop=True)
                    if g == after[0] - 1:
                        pe.wait_ge(loaded["small"], 7 * 16)
                        pe.wait_ge(zeroed, ALL_ZEROED)
                        for h in range(16):
                            nc.tensor.matmul(M.ps[0:DC, 6, h:h + 1], wv[:, h, :], bq[:, h:h + 1],
                                             start=True, stop=True)
                        for m in range(4):
                            last = nc.tensor.matmul(M.ps[:, 7, m * D:(m + 1) * D], ones[:, :], bo[:, m, :],
                                                    start=True, stop=True)
                    last.then_inc(prod, 1)
                pe.wait_ge(wq_ready, 2)
                pe.wait_ge(evac, len(groups))
                for j in range(6):
                    w = IC[j % 3]
                    last = nc.tensor.transpose(M.ps[:, j // 3, (j % 3) * P:(j % 3) * P + w], wi[0:w, j, :],
                                               M.ident[0:w, 0:w])
                for c in range(3):
                    last = nc.tensor.transpose(M.ps[0:IC[c], 2, c * P:(c + 1) * P], wdr[:, c * P:c * P + IC[c]],
                                               M.ident[:, :])
                last.then_inc(prod, 1)

            @block.vector
            def _(dve):
                link = chained(dve, chain)
                dve.wait_ge(loaded["small"], 7 * 16)
                dve.wait_ge(split_done, 2)
                dve.wait_ge(zeroed, ALL_ZEROED)
                nc.vector.tensor_tensor(M.ct_lo[:], cT[:], M.ct_hi[0:DC, :], ALU.subtract)
                nc.vector.tensor_tensor(M.cv_lo[:, :, 0:DC], cV[:], M.cv_hi[:, :, 0:DC], ALU.subtract)
                nc.vector.tensor_copy(M.C[0][0:DC, 1:17, 0:8], wv0[:])
                dve.wait_ge(tanh_done, 1)
                na = 0
                for g, (n, h, kind) in enumerate(groups):
                    L = LAYERS[n]
                    dve.wait_ge(prod, g + 1)
                    if kind == "A":
                        na += 1
                        dve.wait_ge(a_hi, na)
                        nc.vector.scalar_tensor_tensor(
                            M.A_lo[n][:, h:h + 4, :], M.ps[:, g % 6, 0:4 * DC].rearrange("p (h w) -> p h w", h=4),
                            QS * L.scale, M.A_hi[n][:, h:h + 4, :], ALU.mult, ALU.subtract).then_inc(evac, 1)
                    else:
                        nc.vector.tensor_scalar(
                            M.C[n][0:DC, h + 1:h + 5, 0:D], M.ps[0:DC, g % 6, :].rearrange("p (h w) -> p h w", h=4),
                            M.gate[0:DC, n:n + 1], None, ALU.mult).then_inc(evac, 1)
                    if g == after[0] - 1:
                        nc.vector.tensor_scalar(M.qbias[:], M.ps[0:DC, 6, 0:16], QS * L.scale, None, ALU.mult)
                        for m in range(4):
                            nc.vector.tensor_scalar(M.obias[:, m, :], M.ps[:, 7, m * D:(m + 1) * D],
                                                    M.gate[:, m:m + 1], None, ALU.mult)
                dve.wait_ge(loaded["ffn"], 5 * 16)
                for j in range(6):
                    w = IC[j % 3]
                    nc.vector.tensor_reduce(am[0:w, j:j + 1], wn[0:w, j, :], AX.X, ALU.max,
                                            apply_absolute_value=True)
                link(nc.vector.tensor_reduce(am[:, 6:7], wd[:], AX.X, ALU.max, apply_absolute_value=True))
                link(nc.vector.tensor_scalar(sc[:], am[:], 1.0 / QMAX, None, ALU.mult))
                nc.vector.tensor_copy(M.wgs[:], sc[:, 0:3])
                nc.vector.tensor_copy(M.wus[:], sc[:, 3:6])
                link(nc.vector.reciprocal(inv[:, 0:7], sc[:, 0:7]))
                for j in range(6):
                    w = IC[j % 3]
                    nc.vector.tensor_scalar(wr[0:w, j, :], wn[0:w, j, :], inv[0:w, j:j + 1], ROUND,
                                            ALU.mult, ALU.add)
                link(nc.vector.tensor_scalar(wdr[:], wd[:], inv[:, 6:7], ROUND, ALU.mult, ALU.add))
                for j in range(6):
                    w = IC[j % 3]
                    ins = nc.vector.tensor_scalar(wi[0:w, j, :], wr[0:w, j, :], ROUND, None, ALU.subtract)
                ins.then_inc(wq_ready, 1)
                link(nc.vector.tensor_scalar(wdr[:], wdr[:], ROUND, None, ALU.subtract))
                nc.vector.tensor_scalar(wdr[:], wdr[:], sc[:, 6:7], None, ALU.mult).then_inc(wq_ready, 1)
                dve.wait_ge(prod, len(groups) + 1)
                nc.vector.tensor_copy(M.wgq[:], M.ps[:, 0, 0:INTER])
                nc.vector.tensor_copy(M.wuq[:], M.ps[:, 1, 0:INTER])
                for c in range(3):
                    nc.vector.tensor_copy(M.wdT[0:IC[c], c, :], M.ps[0:IC[c], 2, c * P:(c + 1) * P])


def retire(nc, sems):
    for s in sems:
        nc.gpsimd.sem_clear(s)
        nc.release_semaphore(s)


def chained(eng, sem):
    count = [0]

    def link(ins):
        count[0] += 1
        ins.then_inc(sem, 1)
        eng.wait_ge(sem, count[0])

    return link


def layernorm(nc, M, k, split, plain, bias):
    s = M.sem_ln
    with ExitStack() as ctx:
        def sb(name, shape):
            return ctx.enter_context(nc.sbuf_tensor(f"ln{k}_{name}", shape, F32))

        st = sb("stats", [P, NT, 6])
        a, b, c, e = (sb(n, [P, NT]) for n in "abce")
        mean, ve, rstd = sb("mean", [P, NT]), sb("var_eps", [P, NT]), sb("rstd", [P, NT])
        stat0 = k * (NT + 5)
        splits0 = M.splits
        M.splits += split

        with nc.Block() as block:
            @block.vector
            def _(dve):
                for t in range(NT):
                    nc.vector.bn_stats(st[:, t, :], M.x[:, t, :]).then_inc(s["stat"], 1)
                dve.wait_ge(s["stat"], stat0 + NT)
                nc.vector.tensor_tensor(a[:], st[:, :, 1], st[:, :, 4], ALU.add).then_inc(s["stat"], 1)
                nc.vector.tensor_tensor(b[:], st[:, :, 1], st[:, :, 4], ALU.subtract).then_inc(s["stat"], 1)
                nc.vector.tensor_tensor(c[:], st[:, :, 2], st[:, :, 5], ALU.add).then_inc(s["stat"], 1)
                dve.wait_ge(s["stat"], stat0 + NT + 3)
                nc.vector.tensor_scalar(mean[:], a[:], 0.5, None, ALU.mult)
                nc.vector.tensor_tensor(e[:], b[:], b[:], ALU.mult).then_inc(s["stat"], 1)
                nc.vector.tensor_scalar(c[:], c[:], 1.0 / D, EPS, ALU.mult, ALU.add).then_inc(s["stat"], 1)
                dve.wait_ge(s["stat"], stat0 + NT + 5)
                nc.vector.scalar_tensor_tensor(ve[:], e[:], 0.25, c[:], ALU.mult, ALU.add).then_inc(s["var"], 1)
                dve.wait_ge(s["rstd"], k + 1)
                for t in range(NT):
                    nc.vector.tensor_scalar(M.xn[:, t, :], M.x[:, t, :], mean[:, t:t + 1], rstd[:, t:t + 1],
                                            ALU.subtract, ALU.mult).then_inc(s["norm"], 1)
                if split:
                    for q in range(NQ):
                        dve.wait_ge(s["hi"], splits0 * NQ + q + 1)
                        sl = slice(q * QB, (q + 1) * QB)
                        nc.vector.tensor_tensor(M.xt_lo[:, sl], M.ps[:, q, :], M.xt_hi[:, sl], ALU.subtract)

            @block.gpsimd
            def _(pool):
                pool.wait_ge(s["var"], k + 1)
                nc.gpsimd.tensor_tensor(rstd[:], ve[:], M.neghalf[:], ALU.pow).then_inc(s["rstd"], 1)
                if bias is not None:
                    pool.wait_ge(s["norm"], (k + 1) * NT)
                    nc.gpsimd.tensor_tensor(M.x[:], M.x[:],
                                            M.obias[:, bias:bias + 1, :].to_broadcast([P, NT, D]), ALU.add)

            @block.tensor
            def _(pe):
                for t in range(NT):
                    pe.wait_ge(s["norm"], k * NT + t + 1)
                    ins = nc.tensor.transpose(M.ps[:, t // TQ, (t % TQ) * P:(t % TQ + 1) * P], M.xn[:, t, :],
                                              M.ident[:])
                    if t % TQ == TQ - 1:
                        ins.then_inc(s["transposed"], 1)

            @block.scalar
            def _(act):
                for q in range(NQ):
                    act.wait_ge(s["transposed"], k * NQ + q + 1)
                    sl = slice(q * QB, (q + 1) * QB)
                    if plain:
                        nc.scalar.activation(M.xt[:, sl], M.ps[:, q, :], ACT.Copy)
                    if split:
                        nc.scalar.activation(M.xt_hi[:, sl], M.ps[:, q, :], ACT.Copy).then_inc(s["hi"], 1)


def attention(nc, M, layer):
    L = LAYERS[layer]
    H, wide = L.H, L.wide
    UQ = 8 if wide else 1
    MJ = 16 if wide else 2
    ST = (0, 2)
    UB, MISC, MB = 4, 5, (6, 7)
    CW = L.CW
    ps, A_hi, A_lo, C = M.ps, M.A_hi[layer], M.A_lo[layer], M.C[layer]

    def pieces(qb, u):
        if wide:
            return [(2 * u + i, qb * QB, QB, i * QB, 2 * u + i == 0, 2 * u + i == NT - 1) for i in range(2)]
        return [(2 * (2 * qb + j) + i, (2 * qb + j) * SEQ, SEQ, j * QB + i * SEQ, i == 0, i == 1)
                for j in range(2) for i in range(2)]

    def plan(u, prep):
        if not wide:
            pre, mid = [("o", 0), ("m", 0), ("m", 1)], [("o", 1)]
        else:
            m = iter(range(MJ))
            pre = mid = []
            for v, (a, b) in enumerate(((0, 0), (2, 0), (1, 2), (1, 2), (1, 2), (1, 2), (1, 1), (0, 0))):
                pre, mid = [("m", next(m)) for _ in range(a)], [("m", next(m)) for _ in range(b)]
                if v == 1:
                    pre, mid = [("o", 0)] + pre, mid + [("o", 1)]
                if v == u:
                    break
        keep = lambda jobs: [j for j in jobs if prep or j[0] == "o"]
        return keep(pre), keep(mid)

    def job(h, qb, k, prep):
        if prep:
            return 8 + 4 * (h * NQ + qb) + k
        return 8 + 16 * (H - 1) + 2 * qb + k - 1

    with ExitStack() as ctx:
        def sb(name, shape, dt):
            return ctx.enter_context(nc.sbuf_tensor(f"at{layer}_{name}", shape, dt))

        def sem(name):
            sems.append(nc.alloc_semaphore(f"at{layer}_{name}"))
            return sems[-1]

        sems = []

        q_hi = [sb(f"q_hi{i}", [DA, NTOK], F16) for i in range(2)]
        q_lo = [sb(f"q_lo{i}", [DC, NTOK], F16) for i in range(2)]
        p = [sb(f"p{i}", [P, 2 * QB], F32) for i in range(2)]
        p_hi = [sb(f"p_hi{i}", [P, 2 * QB], F16) for i in range(2)]
        p_lo = [sb(f"p_lo{i}", [P, 2 * QB], F16) for i in range(2)]
        nmax = sb("neg_max", [P, TQ], F16)
        mpart = sb("max_part", [P, 16], F32)
        rden = sb("rden", [P, 2], F32)
        qbias = sb("q_bias", [DC, 16], F32)

        st_ready = sem("scores_ready")
        exp_done = sem("exp_done")
        plo_done = sem("p_lo_done")
        av_done = sem("av_done")
        u_evac = sem("u_evac")
        misc_ready = sem("misc_ready")
        misc_free = sem("misc_free")
        qhi_done = sem("q_hi_done")
        m_ready = sem("m_ready")
        m_free = sem("m_free")
        nmax_done = sem("nmax_done")
        rden_done = sem("rden_done")
        waited = sem("waited")
        qbias_ready = sem("q_bias_ready")

        def each_head(eng, head):
            with eng.Fori(0, H // 2 - 1) as i:
                for hh in range(2):
                    head(i * 2 + hh, hh, True, False)
            head(H - 2, 0, True, False)
            head(H - 1, 1, False, True)

        o_sb = [sb(f"o{i}", [P, TQ, 8], F32) for i in range(2)] if layer == 0 else None
        o_stored = [sem(f"o_stored{i}") for i in range(2)]

        with nc.Block() as block:
            if layer == 0:
                @block.sync
                def _(sp):
                    def out(h, qb, idx):
                        sp.wait_ge(misc_free, idx + 2)
                        tokens = slice((qb + NQ - 1) % NQ * QB, ((qb + NQ - 1) % NQ + 1) * QB)
                        sp.dma_start(M.o_dram[h if qb == 0 else h + 1, tokens, :].rearrange("(t p) d -> p t d", p=P),
                                     o_sb[qb % 2][:]).then_inc(o_stored[qb % 2], 16)

                    def head(h, hh, prep, last):
                        for qb in range(NQ):
                            out(h, qb, job(h, qb, 2, prep))

                    each_head(sp, head)
                    out(H, 0, job(H - 1, NQ, 2, False))
                    sp.wait_ge(o_stored[0], (2 * H + 1) * 16 + 16)
                    sp.wait_ge(o_stored[1], 2 * H * 16 + 16)

            @block.tensor
            def _(pe):
                def queries(h, buf, qb, idx):
                    pe.wait_ge(misc_free, idx + 1)
                    sl = slice(qb * QB, (qb + 1) * QB)
                    nc.tensor.matmul(ps[0:DC, MISC, :], A_hi[:, h, :], M.xt_hi[:, sl], start=True, stop=False)
                    nc.tensor.matmul(ps[0:DC, MISC, :], A_hi[:, h, :], M.xt_lo[:, sl], start=False, stop=False)
                    nc.tensor.matmul(ps[0:DC, MISC, :], A_lo[:, h, :], M.xt_hi[:, sl], start=False, stop=True
                                     ).then_inc(misc_ready, 1)

                def maxscores(blk, buf, qb, k):
                    pe.wait_ge(m_free, blk * MJ + k + 1)
                    bank = MB[k % 2]
                    if wide:
                        t, kb = divmod(k, NQ)
                        q0 = qb * QB + t * P
                        ins = nc.tensor.matmul(ps[:, bank, :], q_hi[buf][0:DC, q0:q0 + P],
                                               M.ct_hi[0:DC, kb * QB:(kb + 1) * QB], start=True, stop=True)
                    else:
                        k0 = (2 * qb + k) * SEQ
                        for t in range(2):
                            ins = nc.tensor.matmul(ps[:, bank, t * SEQ:(t + 1) * SEQ],
                                                   q_hi[buf][0:DC, k0 + t * P:k0 + (t + 1) * P],
                                                   M.ct_hi[0:DC, k0:k0 + SEQ], start=True, stop=True)
                    ins.then_inc(m_ready, 1)

                def maxrow(blk, idx):
                    pe.wait_ge(nmax_done, blk + 1)
                    pe.wait_ge(misc_free, idx + 1)
                    for t in range(TQ):
                        ins = nc.tensor.matmul(ps[0:1, MISC, t * P:(t + 1) * P], nmax[:, t:t + 1], M.ident16[:],
                                               start=True, stop=True)
                    ins.then_inc(misc_ready, 1)

                def scores(buf, par, qb, u):
                    for c, q0, nq, at, _, _ in pieces(qb, u):
                        o = ps[:, ST[par] + at // QB, at % QB:at % QB + nq]
                        ks = slice(c * P, (c + 1) * P)
                        nc.tensor.matmul(o, M.ct_hi[:, ks], q_hi[buf][:, q0:q0 + nq], start=True, stop=False)
                        nc.tensor.matmul(o, M.ct_lo[:, ks], q_hi[buf][0:DC, q0:q0 + nq], start=False, stop=False)
                        ins = nc.tensor.matmul(o, M.ct_hi[0:DC, ks], q_lo[buf][:, q0:q0 + nq],
                                               start=False, stop=True)
                    ins.then_inc(st_ready, 1)

                def values(par, qb, u, half):
                    part = pieces(qb, u)
                    part = part[half * len(part) // 2:(half + 1) * len(part) // 2]
                    for c, q0, nq, at, first, last in part:
                        o = ps[:, UB, q0 - qb * QB:q0 - qb * QB + nq]
                        cols = slice(at, at + nq)
                        nc.tensor.matmul(o, M.cv_hi[:, c, :], p_hi[par][:, cols], start=first, stop=False)
                        nc.tensor.matmul(o, M.cv_lo[:, c, :], p_hi[par][:, cols], start=False, stop=False)
                        ins = nc.tensor.matmul(o, M.cv_hi[:, c, :], p_lo[par][:, cols], start=False, stop=last)
                    if half:
                        ins.then_inc(av_done, 1)

                def project(blk, upar, slot, half, idx):
                    pe.wait_ge(misc_free, idx + 1)
                    if half == 0:
                        pe.wait_ge(u_evac, blk + 1)
                    for t in range(2):
                        ins = nc.tensor.matmul(ps[:, MISC, t * (CW + 1):(t + 1) * (CW + 1)],
                                               M.U[:, upar, (2 * half + t) * P:(2 * half + t + 1) * P],
                                               C[:, slot, :], start=True, stop=True)
                    ins.then_inc(misc_ready, 1)

                def head(h, hh, prep, last):
                    for qb in range(NQ):
                        blk = h * NQ + qb
                        for u in range(UQ):
                            n = blk * UQ + u
                            par = (qb * UQ + u) % 2
                            if prep and u == 0:
                                queries(h + 1, 1 - hh, qb, job(h, qb, 0, prep))
                            final = last and qb == NQ - 1 and u == UQ - 1
                            if not final:
                                pe.wait_ge(exp_done, 2 * n + 2)
                                nu = (u + 1) % UQ
                                nq = (qb + (nu == 0)) % NQ
                                nh = 1 - hh if nu == 0 and nq == 0 else hh
                                scores(nh, 1 - par, nq, nu)
                            pre, mid = plan(u, prep)
                            for part, jobs in enumerate((pre, mid)):
                                for kind, k in jobs:
                                    if kind == "m":
                                        maxscores((h + 1) * NQ + qb, 1 - hh, qb, k)
                                    else:
                                        project(blk, (qb + 1) % 2, h if qb == 0 else h + 1, k,
                                                job(h, qb, 1 + k, prep))
                                if part == 0:
                                    pe.wait_ge(plo_done, n + 1)
                                    if u == 0:
                                        pe.wait_ge(u_evac, blk + 1)
                                values(par, qb, u, part)
                        if prep:
                            maxrow((h + 1) * NQ + qb, job(h, qb, 3, prep))

                for qb in range(NQ):
                    queries(0, 0, qb, 2 * qb)
                    pe.wait_ge(misc_free, 2 * qb + 2)
                    for k in range(MJ):
                        maxscores(qb, 0, qb, k)
                    maxrow(qb, 2 * qb + 1)
                pe.wait_ge(misc_free, 2 * NQ + 1)
                scores(0, 0, 0, 0)
                each_head(pe, head)
                for half in range(2):
                    project(H * NQ, 1, H, half, job(H - 1, NQ, 1 + half, False))

            @block.scalar
            def _(act):
                act.sem_inc(exp_done, 2)

                def queries(h, buf, qb, idx):
                    act.wait_ge(misc_ready, idx + 1)
                    o = q_hi[buf][0:DC, qb * QB:(qb + 1) * QB]
                    if layer == 0:
                        act.wait_ge(qbias_ready, 1)
                        act.sem_inc(waited, 1)
                        nc.scalar.activation(o, ps[0:DC, MISC, :], ACT.Identity, bias=qbias[:, bass.ds(h, 1)]
                                             ).then_inc(qhi_done, 1)
                    else:
                        nc.scalar.activation(o, ps[0:DC, MISC, :], ACT.Copy).then_inc(qhi_done, 1)

                def maxrow(buf, qb, idx):
                    act.wait_ge(misc_ready, idx + 1)
                    nc.scalar.activation(q_hi[buf][DC:DA, qb * QB:(qb + 1) * QB], ps[0:1, MISC, :], ACT.Copy
                                         ).then_inc(misc_free, 1)

                def exps(n, par):
                    act.wait_ge(st_ready, n + 1)
                    act.wait_ge(av_done, n + 1)
                    s = ps[:, ST[par]:ST[par] + 2, :]
                    nc.scalar.activation(p[par][:].rearrange("p (b q) -> p b q", b=2), s, ACT.Exp,
                                         scale=1.0 / QS).then_inc(exp_done, 1)
                    nc.scalar.activation(p_hi[par][:].rearrange("p (b q) -> p b q", b=2), s, ACT.Exp,
                                         scale=1.0 / QS).then_inc(exp_done, 1)

                def head(h, hh, prep, last):
                    for qb in range(NQ):
                        blk = h * NQ + qb
                        for u in range(UQ):
                            n = blk * UQ + u
                            par = (qb * UQ + u) % 2
                            if prep and u == 0:
                                queries(h + 1, 1 - hh, qb, job(h, qb, 0, prep))
                            if not (last and qb == NQ - 1 and u == UQ - 1):
                                exps(n + 1, 1 - par)
                        act.wait_ge(av_done, n + 3)
                        before = job(h, qb - 1, 2, prep) if qb or prep else job(h - 1, NQ - 1, 2, True)
                        act.wait_ge(misc_ready, before + 1)
                        nc.scalar.activation(M.U[:, qb % 2, :], ps[0:DA, UB, :], ACT.Copy).then_inc(u_evac, 1)
                        if prep:
                            maxrow(1 - hh, qb, job(h, qb, 3, prep))

                for qb in range(NQ):
                    queries(0, 0, qb, 2 * qb)
                    maxrow(0, qb, 2 * qb + 1)
                exps(0, 0)
                each_head(act, head)

            @block.gpsimd
            def _(pool):
                pool.sem_inc(av_done, 2)
                pool.sem_inc(u_evac, 1)
                pool.sem_inc(misc_free, 1)
                pool.sem_inc(m_free, 2)
                pool.sem_inc(o_stored[0], 16)
                pool.sem_inc(o_stored[1], 16)
                if layer == 0:
                    nc.gpsimd.tensor_copy(qbias[:], M.qbias[:]).then_inc(qbias_ready, 1)

            @block.vector
            def _(dve):
                def queries(h, buf, qb, blk):
                    dve.wait_ge(qhi_done, blk + 1)
                    sl = slice(qb * QB, (qb + 1) * QB)
                    if layer == 0:
                        nc.vector.scalar_tensor_tensor(q_lo[buf][:, sl], ps[0:DC, MISC, :],
                                                       M.qbias[:, bass.ds(h, 1)], q_hi[buf][0:DC, sl],
                                                       ALU.add, ALU.subtract).then_inc(misc_free, 1)
                    else:
                        nc.vector.tensor_tensor(q_lo[buf][:, sl], ps[0:DC, MISC, :], q_hi[buf][0:DC, sl],
                                                ALU.subtract).then_inc(misc_free, 1)

                def maxscores(blk, k):
                    dve.wait_ge(m_ready, blk * MJ + k + 1)
                    if wide:
                        nc.vector.tensor_reduce(mpart[:, k:k + 1], ps[:, MB[k % 2], :], AX.X, ALU.max
                                                ).then_inc(m_free, 1)
                        if k == MJ - 1:
                            dve.wait_ge(m_free, (blk + 1) * MJ + 2)
                            nc.vector.tensor_reduce(nmax[:], mpart[:].rearrange("p (t k) -> p t k", t=TQ), AX.X,
                                                    ALU.max, negate=True).then_inc(nmax_done, 1)
                    else:
                        ins = nc.vector.tensor_reduce(nmax[:, 2 * k:2 * k + 2],
                                                      ps[:, MB[k % 2], :].rearrange("p (t k) -> p t k", t=2),
                                                      AX.X, ALU.max, negate=True).then_inc(m_free, 1)
                        if k == MJ - 1:
                            dve.wait_ge(m_free, (blk + 1) * MJ + 2)
                            dve.sem_inc(nmax_done, 1)

                def project(blk, qb, half, idx, slot, before):
                    dve.wait_ge(misc_ready, idx + 1)
                    v = ps[:, MISC, 0:2 * (CW + 1)].rearrange("p (t w) -> p t w", t=2)
                    nc.vector.reciprocal(rden[:].unsqueeze(2), v[:, :, CW:CW + 1]).then_inc(rden_done, 1)
                    dve.wait_ge(rden_done, blk * 2 + half + 1)
                    if layer == 0 and half == 0:
                        dve.wait_ge(o_stored[(qb + 1) % 2], before * 16 + 16)
                    for t in range(2):
                        tile = qb * TQ + 2 * half + t
                        if layer == 0:
                            ins = nc.vector.scalar_tensor_tensor(
                                o_sb[(qb + 1) % 2][:, 2 * half + t, :], v[:, t, 0:CW], rden[:, t:t + 1],
                                M.vbias[:, slot, :], ALU.mult, ALU.add)
                        else:
                            ins = nc.vector.scalar_tensor_tensor(M.x[:, tile, :], v[:, t, 0:CW], rden[:, t:t + 1],
                                                                 M.x[:, tile, :], ALU.mult, ALU.add)
                    ins.then_inc(misc_free, 1)

                def lows(n, par):
                    dve.wait_ge(exp_done, 2 * n + 4)
                    nc.vector.tensor_tensor(p_lo[par][:], p[par][:], p_hi[par][:], ALU.subtract
                                            ).then_inc(plo_done, 1)

                def head(h, hh, prep, last):
                    for qb in range(NQ):
                        blk = h * NQ + qb
                        for u in range(UQ):
                            n = blk * UQ + u
                            par = (qb * UQ + u) % 2
                            if prep and u == 0:
                                queries(h + 1, 1 - hh, qb, (h + 1) * NQ + qb)
                            pre, mid = plan(u, prep)
                            for kind, k in pre + mid:
                                if kind == "m":
                                    maxscores((h + 1) * NQ + qb, k)
                                else:
                                    project(blk, (qb + NQ - 1) % NQ, k, job(h, qb, 1 + k, prep),
                                            h if qb == 0 else h + 1, h * 2 + qb // 2)
                            if not (last and qb == NQ - 1 and u == UQ - 1):
                                lows(n + 1, 1 - par)

                for qb in range(NQ):
                    queries(0, 0, qb, qb)
                    for k in range(MJ):
                        maxscores(qb, k)
                lows(0, 0)
                each_head(dve, head)
                for half in range(2):
                    project(H * NQ, NQ - 1, half, job(H - 1, NQ, 1 + half, False), H, 2 * H)
        retire(nc, sems)


def gathered_projection(nc, M):
    gathered = [nc.alloc_semaphore(f"gp_gathered{q}") for q in range(NQ)]
    transposed, evac, y_ready = (nc.alloc_semaphore(f"gp_{k}") for k in ("transposed", "evacuated", "y_ready"))
    with nc.Block() as block:
        @block.sync
        def _(sp):
            for t in range(NT):
                b, eight = t // 2, t % 2
                src = M.o_dram[1 + 8 * eight:9 + 8 * eight, b * SEQ:(b + 1) * SEQ, :]
                for h in range(8):
                    sp.dma_start(M.xn[16 * h:16 * h + 16, t, :], src[h].rearrange("(i r) d -> i (r d)", r=16)
                                 ).then_inc(gathered[t // TQ], 16)

        @block.tensor
        def _(pe):
            for q in range(NQ):
                pe.wait_ge(gathered[q], 8 * TQ * 16)
                for t in range(q * TQ, (q + 1) * TQ):
                    ins = nc.tensor.transpose(M.ps[:, q, (t % TQ) * P:(t % TQ + 1) * P], M.xn[:, t, :], M.ident[:])
                ins.then_inc(transposed, 1)
            for q in range(NQ):
                pe.wait_ge(evac, q + 1)
                for t in range(q * TQ, (q + 1) * TQ):
                    ins = nc.tensor.matmul(M.ps[:, 4 + q, (t % TQ) * D:(t % TQ + 1) * D],
                                           M.xt[:, t * P:(t + 1) * P], M.wo0[:], start=True, stop=True)
                ins.then_inc(y_ready, 1)

        @block.scalar
        def _(act):
            for q in range(NQ):
                act.wait_ge(transposed, q + 1)
                nc.scalar.activation(M.xt[:, q * QB:(q + 1) * QB], M.ps[:, q, :], ACT.Copy).then_inc(evac, 1)

        @block.vector
        def _(dve):
            for q in range(NQ):
                dve.wait_ge(y_ready, q + 1)
                tiles = M.x[:, q * TQ:(q + 1) * TQ, :].rearrange("p t f -> p (t f)")
                nc.vector.scalar_tensor_tensor(tiles, M.ps[:, 4 + q, :], M.gate[:, 0:1], tiles, ALU.mult, ALU.add)
    retire(nc, [*gathered, transposed, evac, y_ready])


def quantised_ffn(nc, M):
    with ExitStack() as ctx:
        def sb(name, shape, dt=F32):
            return ctx.enter_context(nc.sbuf_tensor(f"qf_{name}", shape, dt))

        def sem(name):
            sems.append(nc.alloc_semaphore(f"qf_{name}"))
            return sems[-1]

        sems = []

        xq = sb("x_int", [P, NTOK], BF16)
        tmp = sb("tmp", [P, NTOK])
        h = sb("hidden", [P, 3, NTOK])
        gated = [sb(f"gated{i}", [P, QB]) for i in range(2)]
        sig = sb("sigmoid", [P, 2])
        mx, mall, sx, inv = sb("max", [P, 1]), sb("max_all", [P, 1]), sb("scale_x", [P, 1]), sb("inv_x", [P, 1])
        hm, hall, sh, invh = sb("hmax", [P, 3]), sb("hmax_all", [P, 3]), sb("scale_h", [P, 2]), sb("inv_h", [P, 1])
        gs, us, sd = sb("gate_scale", [P, 3]), sb("up_scale", [P, 3]), sb("down_scale", [P, 1])
        chain, sig_ready, exp_done = sem("chain"), sem("clip_ready"), sem("clip_exp")
        xmax, xmax_all, xq_done = sem("x_max"), sem("x_max_all"), sem("x_int_done")
        gate_ready, up_ready, silu_done, h_done = sem("gate_ready"), sem("up_ready"), sem("silu_done"), sem("h_done")
        hmax, hmax_all, hq_done, y_ready = sem("h_max"), sem("h_max_all"), sem("h_int_done"), sem("y_ready")
        jobs = [(q, c) for q in range(NQ) for c in range(3)]

        with nc.Block() as block:
            @block.scalar
            def _(act):
                nc.scalar.activation(sig[:], M.clip[:], ACT.Exp, scale=-1.0).then_inc(exp_done, 1)
                for k, (q, c) in enumerate(jobs):
                    w = IC[c]
                    act.wait_ge(gate_ready, k + 1)
                    if k >= 2:
                        act.wait_ge(h_done, k - 1)
                    nc.scalar.activation(gated[k % 2][0:w, :], M.ps[0:w, k % 4, :], ACT.Silu,
                                         scale=gs[0:w, c:c + 1]).then_inc(silu_done, 1)

            @block.gpsimd
            def _(pool):
                pool.wait_ge(xmax, 1)
                nc.gpsimd.partition_all_reduce(mall[:], mx[:], P, RMAX).then_inc(xmax_all, 1)
                pool.wait_ge(hmax, 1)
                nc.gpsimd.partition_all_reduce(hall[:], hm[:], P, RMAX).then_inc(hmax_all, 1)

            @block.vector
            def _(dve):
                link = chained(dve, chain)
                nc.vector.tensor_reduce(mx[:], M.xt[:], AX.X, ALU.max, apply_absolute_value=True
                                        ).then_inc(xmax, 1)
                nc.vector.memset(hm[:], 0.0)
                dve.wait_ge(exp_done, 1)
                link(nc.vector.tensor_scalar(sig[:], sig[:], 1.0, QMAX, ALU.add, ALU.mult))
                link(nc.vector.reciprocal(sig[:], sig[:]))
                dve.wait_ge(xmax_all, 1)
                link(nc.vector.tensor_tensor(sx[:], mall[:], sig[:, 0:1], ALU.mult))
                nc.vector.tensor_scalar(gs[:], M.wgs[:], sx[:, 0:1], None, ALU.mult)
                nc.vector.tensor_scalar(us[:], M.wus[:], sx[:, 0:1], None, ALU.mult)
                link(nc.vector.reciprocal(inv[:], sx[:]))
                link(nc.vector.tensor_scalar(tmp[:], M.xt[:], inv[:, 0:1], ROUND, ALU.mult, ALU.add))
                link(nc.vector.tensor_scalar(tmp[:], tmp[:], ROUND, QMAX, ALU.subtract, ALU.min))
                nc.vector.tensor_scalar(xq[:], tmp[:], -QMAX - 1.0, None, ALU.max).then_inc(xq_done, 1)
                for k, (q, c) in enumerate(jobs):
                    w = IC[c]
                    dve.wait_ge(silu_done, k + 1)
                    dve.wait_ge(up_ready, k + 1)
                    nc.vector.scalar_tensor_tensor(h[0:w, c, q * QB:(q + 1) * QB], M.ps[0:w, 4 + k % 4, :],
                                                   us[0:w, c:c + 1], gated[k % 2][0:w, :], ALU.mult, ALU.mult
                                                   ).then_inc(h_done, 1)
                dve.wait_ge(h_done, len(jobs))
                for c in range(3):
                    ins = nc.vector.tensor_reduce(hm[0:IC[c], c:c + 1], h[0:IC[c], c, :], AX.X, ALU.max,
                                                  apply_absolute_value=True)
                ins.then_inc(hmax, 1)
                dve.wait_ge(hmax_all, 1)
                link(nc.vector.tensor_reduce(sd[:], hall[:], AX.X, ALU.max))
                link(nc.vector.tensor_tensor(sh[:, 0:1], sd[:], sig[:, 1:2], ALU.mult))
                nc.vector.tensor_tensor(sh[:, 1:2], sh[:, 0:1], M.gate[:, 4:5], ALU.mult)
                link(nc.vector.reciprocal(invh[:], sh[:, 0:1]))
                for c in range(3):
                    w = IC[c]
                    link(nc.vector.tensor_scalar(h[0:w, c, :], h[0:w, c, :], invh[0:w, 0:1], ROUND,
                                                 ALU.mult, ALU.add))
                    link(nc.vector.tensor_scalar(h[0:w, c, :], h[0:w, c, :], ROUND, QMAX, ALU.subtract, ALU.min))
                    nc.vector.tensor_scalar(h[0:w, c, :], h[0:w, c, :], -QMAX - 1.0, None, ALU.max
                                            ).then_inc(hq_done, 1)
                for q in range(NQ):
                    dve.wait_ge(y_ready, q + 1)
                    tiles = M.x[:, q * TQ:(q + 1) * TQ, :].rearrange("p t f -> p (t f)")
                    nc.vector.scalar_tensor_tensor(tiles, M.ps[:, q, :], sh[:, 1:2], tiles, ALU.mult, ALU.add)

            @block.tensor
            def _(pe):
                pe.wait_ge(xq_done, 1)
                for k, (q, c) in enumerate(jobs):
                    w, sl = IC[c], slice(q * QB, (q + 1) * QB)
                    if k >= 4:
                        pe.wait_ge(h_done, k - 3)
                    nc.tensor.matmul(M.ps[0:w, k % 4, :], M.wgq[:, c * P:c * P + w], xq[:, sl],
                                     start=True, stop=True).then_inc(gate_ready, 1)
                    nc.tensor.matmul(M.ps[0:w, 4 + k % 4, :], M.wuq[:, c * P:c * P + w], xq[:, sl],
                                     start=True, stop=True).then_inc(up_ready, 1)
                pe.wait_ge(hq_done, 3)
                for t in range(NT):
                    for c in range(3):
                        w = IC[c]
                        ins = nc.tensor.matmul(M.ps[:, t // TQ, (t % TQ) * D:(t % TQ + 1) * D],
                                               h[0:w, c, t * P:(t + 1) * P], M.wdT[0:w, c, :],
                                               start=c == 0, stop=c == 2)
                    if t % TQ == TQ - 1:
                        ins.then_inc(y_ready, 1)
        retire(nc, sems)


def router(nc, M, d, layer):
    E = (0, 8, 8, 16)[layer]
    with ExitStack() as ctx:
        def sb(name, shape, dt=F32):
            return ctx.enter_context(nc.sbuf_tensor(f"rt{layer}_{name}", shape, dt))

        def sem(name):
            return nc.alloc_semaphore(f"rt{layer}_{name}")

        w = sb("w", [P, E])
        bias = sb("bias", [P, 1, E])
        b2 = sb("b2", [8, D])
        combT = sb("combT", [8, NTOK])
        iota = sb("iota", [P, 1, E])
        v, e, o1, o2, t = (sb(n, [P, NT, E]) for n in ("v", "e", "first", "second", "t"))
        m, m2, i, s, r = (sb(n, [P, NT, 1]) for n in ("m", "m2", "i", "s", "r"))
        loaded, iota_done, logits, chain = sem("loaded"), sem("iota"), sem("logits"), sem("chain")
        shifted, exp_done, comb_done = sem("shifted"), sem("exp"), sem("comb")
        combT_ready, combT_done, b2_ready = sem("combT_ready"), sem("combT_done"), sem("b2_ready")
        nload = {1: 2, 2: 3, 3: 1}[layer]

        def wide(ap):
            return ap.to_broadcast([P, NT, E])

        with nc.Block() as block:
            @block.sync
            def _(sp):
                sp.dma_start(w[:], d[f"L{layer}_router"]).then_inc(loaded, 16)
                if layer < 3:
                    sp.dma_start(bias[:, 0, :], d[f"L{layer}_router_b"]).then_inc(loaded, 16)
                if layer == 2:
                    sp.dma_start(b2[:], d["L2_b2"]).then_inc(loaded, 16)

            @block.gpsimd
            def _(pool):
                for k in range(E):
                    ins = nc.gpsimd.memset(iota[:, :, k:k + 1], float(k - E))
                ins.then_inc(iota_done, 1)

            @block.tensor
            def _(pe):
                pe.wait_ge(loaded, 16 * nload)
                for n in range(NT):
                    ins = nc.tensor.matmul(M.ps[:, 0, n * E:(n + 1) * E], M.xt[:, n * P:(n + 1) * P], w[:],
                                           start=True, stop=True)
                ins.then_inc(logits, 1)
                if layer == 2:
                    pe.wait_ge(comb_done, 1)
                    for n in range(NT):
                        ins = nc.tensor.transpose(M.ps[0:8, 4 + n // TQ, (n % TQ) * P:(n % TQ + 1) * P],
                                                  M.comb[:, n, 0:8], M.ident[:])
                    ins.then_inc(combT_ready, 1)
                    pe.wait_ge(combT_done, 1)
                    for n in range(NT):
                        ins = nc.tensor.matmul(M.ps[:, n // TQ, (n % TQ) * D:(n % TQ + 1) * D],
                                               combT[:, n * P:(n + 1) * P], b2[:], start=True, stop=True)
                    ins.then_inc(b2_ready, 1)

            @block.scalar
            def _(act):
                act.wait_ge(shifted, 1)
                if layer == 2:
                    nc.scalar.activation(s[:], r[:], ACT.Exp).then_inc(exp_done, 1)
                    act.wait_ge(combT_ready, 1)
                    nc.scalar.activation(combT[:].rearrange("e (b t) -> e b t", b=4), M.ps[0:8, 4:8, :], ACT.Copy
                                         ).then_inc(combT_done, 1)
                else:
                    nc.scalar.activation(e[:], e[:], ACT.Exp).then_inc(exp_done, 1)

            @block.vector
            def _(dve):
                link = chained(dve, chain)
                V = nc.vector

                def first_largest(values, top, onehot):
                    link(V.tensor_reduce(top[:], values[:], AX.X, ALU.max))
                    link(V.tensor_tensor(t[:], values[:], wide(top[:]), ALU.is_ge))
                    link(V.tensor_tensor(t[:], t[:], iota[:].to_broadcast([P, NT, E]), ALU.mult))
                    link(V.tensor_reduce(i[:], t[:], AX.X, ALU.min))
                    link(V.tensor_tensor(onehot[:], iota[:].to_broadcast([P, NT, E]), wide(i[:]), ALU.is_equal))

                dve.wait_ge(iota_done, 1)
                dve.wait_ge(logits, 1)
                lg = M.ps[:, 0, 0:NT * E].rearrange("p (n e) -> p n e", n=NT)
                if layer < 3:
                    link(V.tensor_tensor(v[:], lg, bias[:].to_broadcast([P, NT, E]), ALU.add))
                else:
                    link(V.tensor_copy(v[:], lg))
                gate = M.gate[:, 4 + layer:5 + layer]
                if layer != 2:
                    link(V.tensor_reduce(m[:], v[:], AX.X, ALU.max))
                    V.tensor_tensor(e[:], v[:], wide(m[:]), ALU.subtract).then_inc(shifted, 1)
                if layer == 1:
                    first_largest(v, m2, o1)
                    dve.wait_ge(exp_done, 1)
                    link(V.tensor_reduce(s[:], e[:], AX.X, ALU.add))
                    link(V.reciprocal(r[:], s[:]))
                    link(V.tensor_scalar(r[:], r[:], gate, None, ALU.mult))
                    V.tensor_tensor(M.comb[:, :, 0:E], o1[:], wide(r[:]), ALU.mult)
                if layer == 2:
                    first_largest(v, m, o1)
                    link(V.tensor_scalar(e[:], o1[:], -3.0e38, None, ALU.mult))
                    link(V.tensor_tensor(t[:], o1[:], v[:], ALU.mult))
                    link(V.tensor_tensor(v[:], v[:], t[:], ALU.subtract))
                    link(V.tensor_tensor(v[:], v[:], e[:], ALU.add))
                    first_largest(v, m2, o2)
                    V.tensor_tensor(r[:], m2[:], m[:], ALU.subtract).then_inc(shifted, 1)
                    dve.wait_ge(exp_done, 1)
                    link(V.tensor_scalar(m[:], s[:], 1.0, None, ALU.add))
                    link(V.reciprocal(m[:], m[:]))
                    link(V.tensor_scalar(m[:], m[:], gate, None, ALU.mult))
                    link(V.tensor_tensor(m2[:], m[:], s[:], ALU.mult))
                    link(V.tensor_tensor(o1[:], o1[:], wide(m[:]), ALU.mult))
                    link(V.tensor_tensor(o2[:], o2[:], wide(m2[:]), ALU.mult))
                    V.tensor_tensor(M.comb[:, :, 0:E], o1[:], o2[:], ALU.add).then_inc(comb_done, 1)
                    dve.wait_ge(b2_ready, 1)
                    xs = M.x[:].rearrange("p (b t) f -> p b (t f)", b=4)
                    V.tensor_tensor(xs, xs, M.ps[:, 0:4, :], ALU.add)
                if layer == 3:
                    dve.wait_ge(exp_done, 1)
                    link(V.tensor_reduce(s[:], e[:], AX.X, ALU.add))
                    link(V.reciprocal(s[:], s[:]))
                    link(V.tensor_tensor(e[:], e[:], wide(s[:]), ALU.mult))
                    first_largest(e, m, o1)
                    link(V.scalar_tensor_tensor(v[:], o1[:], -2.0, e[:], ALU.mult, ALU.add))
                    first_largest(v, m2, o2)
                    link(V.tensor_tensor(o1[:], o1[:], o2[:], ALU.add))
                    link(V.tensor_tensor(o1[:], o1[:], e[:], ALU.mult))
                    V.tensor_scalar(M.comb[:, :, 0:E], o1[:], gate, None, ALU.mult)
                    link(V.memset(o2[:, :, 0:2], 1.0))
                    V.tensor_scalar(M.comb[:, :, E:E + 2], o2[:, :, 0:2], gate, None, ALU.mult)


def expert_ffn(nc, M, d, layer):
    E, FC, two, gated = {1: (8, 4, False, True), 2: (8, 4, False, False), 3: (9, 1, True, True)}[layer]
    W = FC * P * (2 if gated else 1)
    NA, NG, NY = (2, 4, 2) if not two else (2, 2, 2)
    if not gated:
        NA, NG = 4, 0
    YB = NA + NG
    YW = 2 if two else 1
    ps = M.ps

    with ExitStack() as ctx:
        def sb(name, shape, dt=F32):
            return ctx.enter_context(nc.sbuf_tensor(f"ex{layer}_{name}", shape, dt))

        def sem(name):
            sems.append(nc.alloc_semaphore(f"ex{layer}_{name}"))
            return sems[-1]

        sems = []

        raw = [sb(f"w1_raw{i}", [P, W]) for i in range(2)]
        w_hi = [sb(f"w1_hi{i}", [P, W], F16) for i in range(2)]
        w_lo = [sb(f"w1_lo{i}", [P, W], F16) for i in range(2)]
        w2 = [sb(f"w2_{i}", [P, FC, D]) for i in range(2)]
        hid = [sb(f"hidden{i}", [P, FC, QB]) for i in range(2)]
        act_out = [sb(f"silu{i}", [P, QB]) for i in range(2)]
        b1 = sb("b1", [P, 8 * FC])
        b1_loaded = sem("b1_loaded")
        waited = sem("waited")
        w1_loaded, w2_loaded = [sem(f"w1_loaded{i}") for i in range(2)], [sem(f"w2_loaded{i}") for i in range(2)]
        w1_hi_done = sem("w1_hi_done")
        w1_done = sem("w1_split")
        a_ready, g_ready = sem("a_ready"), sem("g_ready")
        silu_done = sem("silu_done")
        hid_done = sem("hid_done")
        y_ready = sem("y_ready")
        half_done = sem("half_done")
        y_done = sem("y_done")
        NH = NG if gated else NA

        def each_expert(eng, expert):
            n = (E - 1) // 2
            with eng.Fori(0, n) as i:
                for j in range(2):
                    expert(i * 2 + j, j, False, i)
            for e in range(2 * n, E):
                expert(e, e % 2, e == E - 1, e // 2)

        with nc.Block() as block:
            @block.sync
            def _(sp):
                if not gated:
                    sp.dma_start(b1[:], d["L2_b1"]).then_inc(b1_loaded, 16)

                def load(e, j, last, times):
                    sp.wait_ge(w1_done, e + 1)
                    sp.dma_start(raw[j][:], d[f"L{layer}_w1"][e]).then_inc(w1_loaded[j], 16)
                    sp.wait_ge(y_ready, e * NQ + NQ)
                    sp.dma_start(w2[j][:], d[f"L{layer}_w2"][e].rearrange("(f p) n -> p f n", p=P)
                                 ).then_inc(w2_loaded[j], 16)

                each_expert(sp, load)

            @block.gpsimd
            def _(pool):
                pool.sem_inc(w1_done, 2)
                pool.sem_inc(silu_done, NA)
                pool.sem_inc(hid_done, NH)
                pool.sem_inc(y_ready, 2 * NQ)
                pool.sem_inc(y_done, 2)

                def split(e, j, last, times):
                    pool.wait_ge(w1_loaded[j], times * 16 + 16)
                    pool.wait_ge(y_ready, e * NQ + NQ)
                    nc.gpsimd.tensor_tensor(w_hi[j][:], raw[j][:], M.one[:].to_broadcast([P, W]), ALU.mult
                                            ).then_inc(w1_hi_done, 1)
                    pool.wait_ge(w1_hi_done, e + 1)
                    nc.gpsimd.tensor_tensor(w_lo[j][:], raw[j][:], w_hi[j][:], ALU.subtract).then_inc(w1_done, 1)

                each_expert(pool, split)

            def each_step(e, j, last):
                for q in range(NQ):
                    end = last and q == NQ - 1
                    ne, nj, nq = (e, j, q + 1) if q < NQ - 1 else (e + 1, 1 - j, 0)
                    yield q, e * NQ + q, end, ne, nj, nq

            @block.tensor
            def _(pe):
                def chunk(j, q, f, k, kk):
                    sl = slice(q * QB, (q + 1) * QB)

                    def product(bank, at):
                        nc.tensor.matmul(ps[:, bank, :], w_hi[j][:, at:at + P], M.xt_hi[:, sl],
                                         start=True, stop=False)
                        nc.tensor.matmul(ps[:, bank, :], w_lo[j][:, at:at + P], M.xt_hi[:, sl],
                                         start=False, stop=False)
                        return nc.tensor.matmul(ps[:, bank, :], w_hi[j][:, at:at + P], M.xt_lo[:, sl],
                                                start=False, stop=True)

                    pe.wait_ge(silu_done if gated else hid_done, k + 1)
                    product(kk % NA, f * P).then_inc(a_ready, 1)
                    if gated:
                        pe.wait_ge(hid_done, k + 1)
                        product(NA + kk % NG, (FC + f) * P).then_inc(g_ready, 1)

                def result(j, n, nn, times):
                    pe.wait_ge(y_done, n + 1)
                    pe.wait_ge(hid_done, (n + 1) * FC + NH)
                    if nn % NQ == 0:
                        pe.wait_ge(w2_loaded[j], times * 16 + 16)
                    y = YB + (nn % NY) * YW
                    for t in range(TQ):
                        if two:
                            for r in range(2):
                                ins = nc.tensor.matmul(ps[:, y + r, t * D:(t + 1) * D],
                                                       hid[nn % 2][64 * r:64 * r + 64, 0, t * P:(t + 1) * P],
                                                       w2[j][64 * r:64 * r + 64, 0, :], start=True, stop=True)
                        else:
                            for f in range(FC):
                                ins = nc.tensor.matmul(ps[:, y, t * D:(t + 1) * D],
                                                       hid[nn % 2][:, f, t * P:(t + 1) * P], w2[j][:, f, :],
                                                       start=f == 0, stop=f == FC - 1)
                    ins.then_inc(y_ready, 1)

                def expert(e, j, last, times):
                    for q, n, end, ne, nj, nq in each_step(e, j, last):
                        for f in range(1, FC):
                            chunk(j, q, f, n * FC + f, q * FC + f)
                        if not end:
                            if nq == 0:
                                pe.wait_ge(w1_done, ne + 3)
                            chunk(nj, nq, 0, (n + 1) * FC, nq * FC)
                        result(j, n, q, times)

                pe.wait_ge(w1_done, 3)
                chunk(0, 0, 0, 0, 0)
                each_expert(pe, expert)

            @block.scalar
            def _(act):
                def chunk(e, q, f, n, k, kk):
                    act.wait_ge(a_ready, k + 1)
                    if gated:
                        act.wait_ge(hid_done, k - 1 + NH)
                        nc.scalar.activation(act_out[kk % 2][:], ps[:, kk % NA, :], ACT.Silu).then_inc(silu_done, 1)
                    else:
                        if f == 0:
                            act.wait_ge(y_ready, n + 2 * NQ - 1)
                        act.wait_ge(b1_loaded, 16)
                        act.sem_inc(waited, 1)
                        nc.scalar.activation(hid[q % 2][:, f, :], ps[:, kk % NA, :], ACT.Gelu,
                                             bias=b1[:, bass.ds(e * FC + f, 1)]).then_inc(hid_done, 1)

                def expert(e, j, last, times):
                    for q, n, end, ne, nj, nq in each_step(e, j, last):
                        for f in range(1, FC):
                            chunk(e, q, f, n, n * FC + f, q * FC + f)
                        if not end:
                            chunk(ne, nq, 0, n + 1, (n + 1) * FC, nq * FC)

                chunk(0, 0, 0, 0, 0, 0)
                each_expert(act, expert)

            @block.vector
            def _(dve):
                def chunk(q, f, n, k, kk):
                    if not gated:
                        return
                    if f == 0:
                        dve.wait_ge(y_ready, n + 2 * NQ - 1)
                    dve.wait_ge(silu_done, k + 1 + NA)
                    dve.wait_ge(g_ready, k + 1)
                    nc.vector.tensor_tensor(hid[q % 2][:, f, :], ps[:, NA + kk % NG, :], act_out[kk % 2][:],
                                            ALU.mult).then_inc(hid_done, 1)

                def result(e, q, n):
                    dve.wait_ge(y_ready, n + 1 + 2 * NQ)
                    y = YB + (q % NY) * YW
                    for r in range(YW):
                        for t in range(TQ):
                            tile = q * TQ + t
                            ins = nc.vector.scalar_tensor_tensor(
                                M.x[:, tile, :], ps[:, y + r, t * D:(t + 1) * D],
                                M.comb[:, tile, bass.ds(e * YW + r, 1)], M.x[:, tile, :], ALU.mult, ALU.add)
                            if r == 0 and two:
                                ins.then_inc(half_done, 1)
                        if r == 0 and two:
                            dve.wait_ge(half_done, (n + 1) * TQ)
                    ins.then_inc(y_done, 1)

                def expert(e, j, last, times):
                    for q, n, end, ne, nj, nq in each_step(e, j, last):
                        for f in range(1, FC):
                            chunk(q, f, n, n * FC + f, q * FC + f)
                        if not end:
                            chunk(nq, 0, n + 1, (n + 1) * FC, nq * FC)
                        result(e, q, n)

                chunk(0, 0, 0, 0, 0)
                each_expert(dve, expert)
        retire(nc, sems)


def store(nc, M, out):
    stored = nc.alloc_semaphore("stored")
    with nc.Block() as block:
        @block.sync
        def _(sp):
            sp.dma_start(out.rearrange("b (t p) f -> p (b t) f", p=P), M.x[:]).then_inc(stored, 16)
            sp.wait_ge(stored, 16)


def kernel(**inputs):
    import concourse.bacc as bacc
    from concourse.bass_utils import run_bass_kernel_spmd

    a = {k: np.asarray(v) for k, v in inputs.items()}
    heads = lambda w, n, h: w.reshape(n, h, -1).transpose(1, 0, 2)
    dims = [(L.H, L.DH) for L in LAYERS]
    lay = {
        "x": a["x"].reshape(NTOK, D),
        "ctx": a["ctx_768"].reshape(NTOK, DC),
        "ctxT": a["ctx_768"].reshape(NTOK, DC).T,
        "g": np.broadcast_to(np.concatenate([a["g_xattn"], a["g_ffn"]]), (P, 8)),
        "clip": np.broadcast_to(np.concatenate([a["L0_ffn_clip_x"], a["L0_ffn_clip_down"]]), (P, 2)),
        "L0_q": heads(a["L0_xattn_q_w"], *dims[0]), "L0_k": heads(a["L0_xattn_v_w"], *dims[0]),
        "L0_wv": a["L0_xattn_v_w"].T.reshape(DC, 16, 8), "L0_wo": a["L0_xattn_o_w"].T,
        "L0_bq": a["L0_xattn_q_b"].reshape(16, 8).T,
        "L0_bv": np.broadcast_to(a["L0_xattn_v_b"].reshape(1, 16, 8), (P, 16, 8)),
        "bo": np.stack([a["L0_xattn_o_b"], a["L1_xattn_bo"], a["L2_xattn_bout"], a["L3_xattn_b_out"]])[None],
        "L0_gate": a["L0_ffn_w_gate"], "L0_up": a["L0_ffn_w_up"], "L0_down": a["L0_ffn_w_down"],
        "L1_q": heads(a["L1_xattn_Wq"].T, *dims[1]), "L1_k": heads(a["L1_xattn_Wk"].T, *dims[1]),
        "L1_v": heads(a["L1_xattn_Wv"].T, *dims[1]), "L1_o": heads(a["L1_xattn_Wo"], *dims[1]),
        "L1_router": a["L1_ffn_router_w"], "L1_router_b": np.broadcast_to(a["L1_ffn_router_b"], (P, 8)),
        "L1_w1": a["L1_ffn_w1"], "L1_w2": a["L1_ffn_w2"],
        "L2_q": heads(a["L2_xattn_Wq"].T, *dims[2]), "L2_k": heads(a["L2_xattn_Wk"].T, *dims[2]),
        "L2_v": heads(a["L2_xattn_Wv"].T, *dims[2]), "L2_o": heads(a["L2_xattn_Wout"], *dims[2]),
        "L2_router": a["L2_ffn_gate_w"], "L2_router_b": np.broadcast_to(a["L2_ffn_gate_b"], (P, 8)),
        "L2_w1": a["L2_ffn_w1"], "L2_w2": a["L2_ffn_w2"], "L2_b2": a["L2_ffn_b2"],
        "L2_b1": a["L2_ffn_b1"].reshape(8 * 4, P).T,
        "L3_q": heads(a["L3_xattn_w_q"].T, *dims[3]),
        "L3_k": heads(a["L3_xattn_w_kv"][:, :1024].T, *dims[3]),
        "L3_v": heads(a["L3_xattn_w_kv"][:, 1024:].T, *dims[3]),
        "L3_o": heads(a["L3_xattn_w_out"], *dims[3]),
        "L3_router": a["L3_ffn_router_w"],
        "L3_w1": np.concatenate([
            np.concatenate([w.reshape(8, 2, D, 64).transpose(0, 2, 1, 3).reshape(8, D, P), s[None]])
            for w, s in ((a["L3_ffn_gate_w"], a["L3_ffn_shared_gate_w"]), (a["L3_ffn_up_w"], a["L3_ffn_shared_up_w"]))
        ], axis=2),
        "L3_w2": np.concatenate([a["L3_ffn_down_w"].reshape(8, P, D), a["L3_ffn_shared_down_w"][None]]),
    }
    lay = {k: np.ascontiguousarray(v) for k, v in lay.items()}
    nc = bacc.Bacc("TRN2", target_bir_lowering=False, num_devices=1)
    d = {k: nc.dram_tensor(f"in_{k}", v.shape, mybir.dt.from_np(v.dtype), kind="ExternalInput").ap()
         for k, v in lay.items()}
    out = nc.dram_tensor("out", a["x"].shape, F32, kind="ExternalOutput").ap()
    build(nc, d, out)
    r = run_bass_kernel_spmd(nc, [{f"in_{k}": v for k, v in lay.items()}], core_ids=[0])
    return r.results[0]["out"]
```

```python
from collections import namedtuple
from contextlib import ExitStack

import concourse.bass as bass
import numpy as np
from concourse import mybir

F32 = mybir.dt.float32
F16 = mybir.dt.float16
BF16 = mybir.dt.bfloat16
ALU = mybir.AluOpType
ACT = mybir.ActivationFunctionType
AX = mybir.AxisListType
RMAX = bass.bass_isa.ReduceOp.max

P = 128
D = 128
DC = 96
DA = DC + 1
NTOK = 2048
NT = NTOK // P
QB = 512
NQ = NTOK // QB
TQ = QB // P
SEQ = 256
QS = 64.0
EPS = 1e-5
ROUND = 12582912.0
QMAX = 127.0
Layer = namedtuple("Layer", "H DH scale wide CW")
LAYERS = (
    Layer(16, 8, 8 ** -0.5, False, 8),
    Layer(16, 64, 64 ** -0.5, False, D),
    Layer(8, 128, 1.5 * 128 ** -0.5, True, D),
    Layer(16, 64, 64 ** -0.5, False, D),
)
INTER = 352
IC = (128, 128, 96)


def build(nc, d, out):
    with ExitStack() as ctx:
        M = persistent(nc, ctx)
        prepare(nc, M, d)
        for n in range(4):
            layernorm(nc, M, 2 * n, split=True, plain=False, bias=n)
            attention(nc, M, n)
            if n == 0:
                gathered_projection(nc, M)
            layernorm(nc, M, 2 * n + 1, split=n > 0, plain=True, bias=None)
            if n == 0:
                quantised_ffn(nc, M)
            else:
                router(nc, M, d, n)
                expert_ffn(nc, M, d, n)
        store(nc, M, out)


class Memory:
    pass


def persistent(nc, ctx):
    M = Memory()

    def sb(name, shape, dt):
        return ctx.enter_context(nc.sbuf_tensor(name, shape, dt))

    M.x = sb("x_res", [P, NT, D], F32)
    M.xn = sb("x_norm", [P, NT, D], F32)
    M.xt = sb("x_normT", [P, NTOK], F32)
    M.xt_hi = sb("x_normT_hi", [P, NTOK], F16)
    M.xt_lo = sb("x_normT_lo", [P, NTOK], F16)
    M.ct_hi = sb("ctxT_hi", [DA, NTOK], F16)
    M.ct_lo = sb("ctxT_lo", [DC, NTOK], F16)
    M.cv_hi = sb("ctx_hi", [P, NT, P], F16)
    M.cv_lo = sb("ctx_lo", [P, NT, P], F16)
    M.A_hi = [sb(f"A{n}_hi", [P, L.H, DC], F16) for n, L in enumerate(LAYERS)]
    M.A_lo = [sb(f"A{n}_lo", [P, L.H, DC], F16) for n, L in enumerate(LAYERS)]
    M.C = [sb(f"C{n}", [DA, L.H + 1, L.CW + 1], F32) for n, L in enumerate(LAYERS)]
    M.vbias = sb("v_bias", [P, 17, 8], F32)
    M.wo0 = sb("wo0", [P, D], F32)
    M.o_dram = nc.dram_tensor("o_scratch", [17, NTOK, 8], F32, kind="Internal").ap()
    M.qbias = sb("q_bias", [DC, LAYERS[0].H], F32)
    M.obias = sb("out_bias", [P, 4, D], F32)
    M.gate = sb("gates", [P, 8], F32)
    M.ident = sb("ident", [P, P], F32)
    M.ident16 = sb("ident16", [P, P], F16)
    M.neghalf = sb("neg_half", [P, NT], F32)
    M.one = sb("one", [P, 1], F32)
    M.U = sb("u_out", [DA, 2, QB], F32)
    M.wgq = sb("w_gate_q", [P, INTER], BF16)
    M.wuq = sb("w_up_q", [P, INTER], BF16)
    M.wgs = sb("w_gate_s", [P, 3], F32)
    M.wus = sb("w_up_s", [P, 3], F32)
    M.wdT = sb("w_downT", [P, 3, D], F32)
    M.clip = sb("clips", [P, 2], F32)
    M.comb = sb("comb", [P, NT, 18], F32)
    M.ps = ctx.enter_context(nc.psum_tensor("ps", [P, 8, 512], F32))
    M.splits = 0
    M.sem_ln = {k: nc.alloc_semaphore(f"ln_{k}") for k in
                ("stat", "var", "rstd", "norm", "transposed", "hi")}
    return M


def prepare(nc, M, d):
    with ExitStack() as ctx:
        def sb(name, shape, dt):
            return ctx.enter_context(nc.sbuf_tensor(name, shape, dt))

        raw = [sb(f"raw{i}", [P, 16 * (2 * D + 2 * DC)], F32) for i in range(2)]
        cT = sb("ctxT_raw", [DC, NTOK], F32)
        cV = sb("ctx_raw", [P, NT, DC], F32)
        bq = sb("bq", [8, 16], F32)
        wv0 = sb("wv0", [DC, 16, 8], F32)
        bo = sb("bo", [1, 4, D], F32)
        ones = sb("ones_row", [1, P], F32)
        wn = sb("w_nat", [P, 6, D], F32)
        wd = sb("w_down", [P, INTER], F32)
        wr = sb("w_rounded", [P, 6, D], F32)
        wdr = sb("w_down_rounded", [P, INTER], F32)
        wi = sb("w_int", [P, 6, D], F32)
        am = sb("w_absmax", [P, 8], F32)
        sc = sb("w_scale", [P, 8], F32)
        inv = sb("w_inv", [P, 8], F32)

        loaded = {k: nc.alloc_semaphore(f"loaded_{k}") for k in ("x", "ctx", "small", "w0", "w1", "w2", "w3", "ffn")}
        zeroed = nc.alloc_semaphore("prep_zeroed")
        tanh_done = nc.alloc_semaphore("prep_tanh")
        split_done = nc.alloc_semaphore("prep_ctx_split")
        prod = nc.alloc_semaphore("prep_products")
        a_hi = nc.alloc_semaphore("prep_a_hi")
        evac = nc.alloc_semaphore("prep_evacuated")
        chain = nc.alloc_semaphore("prep_chain")
        wq_ready = nc.alloc_semaphore("prep_quantised")

        def views(n):
            L = LAYERS[n]
            r, at, v = raw[n % 2], 0, []
            for w in (D, DC, DC, D):
                v.append(r[0:L.DH, at:at + L.H * w].rearrange("p (h w) -> p h w", h=L.H))
                at += L.H * w
            return v

        names = (("L0_q", "L0_k"), ("L1_q", "L1_k", "L1_v", "L1_o"),
                 ("L2_q", "L2_k", "L2_v", "L2_o"), ("L3_q", "L3_k", "L3_v", "L3_o"))
        groups = [(n, h, kind) for n, L in enumerate(LAYERS) for h in range(0, L.H, 4) for kind in ("AC" if n else "A")]
        after = [sum(1 for g in groups if g[0] <= n) for n in range(4)]

        with nc.Block() as block:
            @block.sync
            def _(sp):
                for n in range(4):
                    if n >= 2:
                        sp.wait_ge(prod, after[n - 2])
                    for v, name in zip(views(n), names[n]):
                        sp.dma_start(v, d[name]).then_inc(loaded[f"w{n}"], 16)
                    if n == 0:
                        sp.dma_start(M.x[:], d["x"].rearrange("(t p) f -> p t f", p=P)).then_inc(loaded["x"], 16)
                sp.wait_ge(loaded["x"], 16)

            @block.scalar
            def _(act):
                for dst, name in ((bq[:], "L0_bq"), (wv0[:], "L0_wv"), (bo[:], "bo"), (M.gate[:], "g"),
                                  (M.clip[:], "clip"), (M.wo0[:], "L0_wo"), (M.vbias[:, 1:17, :], "L0_bv")):
                    act.dma_start(dst, d[name]).then_inc(loaded["small"], 16)
                act.dma_start(cT[:], d["ctxT"]).then_inc(loaded["ctx"], 16)
                act.dma_start(cV[:], d["ctx"].rearrange("(t p) f -> p t f", p=P)).then_inc(loaded["ctx"], 16)
                for j, name in enumerate(("L0_gate", "L0_up")):
                    act.dma_start(wn[:, 3 * j:3 * j + 2, :], d[name][0:2 * P, :].rearrange("(c p) f -> p c f", p=P)
                                  ).then_inc(loaded["ffn"], 16)
                    act.dma_start(wn[0:IC[2], 3 * j + 2, :], d[name][2 * P:INTER, :]).then_inc(loaded["ffn"], 16)
                act.dma_start(wd[:], d["L0_down"]).then_inc(loaded["ffn"], 16)
                act.wait_ge(loaded["small"], 7 * 16)
                nc.scalar.activation(M.gate[:], M.gate[:], ACT.Tanh).then_inc(tanh_done, 1)
                act.wait_ge(loaded["ctx"], 32)
                act.wait_ge(zeroed, 6)
                nc.scalar.activation(M.ct_hi[0:DC, :], cT[:], ACT.Copy).then_inc(split_done, 1)
                nc.scalar.activation(M.cv_hi[:, :, 0:DC], cV[:], ACT.Copy).then_inc(split_done, 1)
                na = 0
                for g, (n, h, kind) in enumerate(groups):
                    if kind == "A":
                        act.wait_ge(prod, g + 1)
                        na += 1
                        nc.scalar.activation(
                            M.A_hi[n][:, h:h + 4, :], M.ps[:, g % 6, 0:4 * DC].rearrange("p (h w) -> p h w", h=4),
                            ACT.Copy, scale=QS * LAYERS[n].scale).then_inc(a_hi, 1)

            @block.gpsimd
            def _(pool):
                link = chained(pool, zeroed)

                def fill(ap, value=0.0):
                    link(nc.gpsimd.memset(ap, value))

                fill(M.ident[:])
                link(nc.gpsimd.affine_select(out=M.ident[:], in_=M.ident[:], compare_op=ALU.not_equal, fill=1.0,
                                             base=0, pattern=[[-1, P]], channel_multiplier=1))
                fill(M.cv_hi[:])
                fill(M.cv_lo[:])
                fill(M.ct_hi[DC:DA, :], 1.0)
                fill(M.cv_hi[:, :, DC:DA], 1.0)
                fill(ones[:], 1.0)
                fill(am[:])
                fill(M.neghalf[:], -0.5)
                fill(M.one[:], 1.0)
                fill(M.U[:, 1, :])
                for n in range(4):
                    fill(M.C[n][:])
                link(nc.gpsimd.tensor_copy(M.ident16[:], M.ident[:]))
                fill(M.U[DC:DA, 1, :], 1.0)
                for n, L in enumerate(LAYERS):
                    fill(M.C[n][DC:DA, :, L.CW:L.CW + 1], 1.0)
                fill(M.vbias[:, 0, :])

            ALL_ZEROED = 22

            @block.tensor
            def _(pe):
                for g, (n, h0, kind) in enumerate(groups):
                    if g == 0 or groups[g - 1][0] != n:
                        pe.wait_ge(loaded[f"w{n}"], 16 * len(names[n]))
                    if g >= 6:
                        pe.wait_ge(evac, g - 5)
                    wq, wk, wv, wo = views(n)
                    wv = wk if n == 0 else wv
                    for j in range(4):
                        h = h0 + j
                        if kind == "A":
                            last = nc.tensor.matmul(M.ps[:, g % 6, j * DC:(j + 1) * DC], wq[:, h, :], wk[:, h, :],
                                                    start=True, stop=True)
                        else:
                            last = nc.tensor.matmul(M.ps[0:DC, g % 6, j * D:(j + 1) * D], wv[:, h, :], wo[:, h, :],
                                                    start=True, stop=True)
                    if g == after[0] - 1:
                        pe.wait_ge(loaded["small"], 7 * 16)
                        pe.wait_ge(zeroed, ALL_ZEROED)
                        for h in range(16):
                            nc.tensor.matmul(M.ps[0:DC, 6, h:h + 1], wv[:, h, :], bq[:, h:h + 1],
                                             start=True, stop=True)
                        for m in range(4):
                            last = nc.tensor.matmul(M.ps[:, 7, m * D:(m + 1) * D], ones[:, :], bo[:, m, :],
                                                    start=True, stop=True)
                    last.then_inc(prod, 1)
                pe.wait_ge(wq_ready, 2)
                pe.wait_ge(evac, len(groups))
                for j in range(6):
                    w = IC[j % 3]
                    last = nc.tensor.transpose(M.ps[:, j // 3, (j % 3) * P:(j % 3) * P + w], wi[0:w, j, :],
                                               M.ident[0:w, 0:w])
                for c in range(3):
                    last = nc.tensor.transpose(M.ps[0:IC[c], 2, c * P:(c + 1) * P], wdr[:, c * P:c * P + IC[c]],
                                               M.ident[:, :])
                last.then_inc(prod, 1)

            @block.vector
            def _(dve):
                link = chained(dve, chain)
                dve.wait_ge(loaded["small"], 7 * 16)
                dve.wait_ge(split_done, 2)
                dve.wait_ge(zeroed, ALL_ZEROED)
                nc.vector.tensor_tensor(M.ct_lo[:], cT[:], M.ct_hi[0:DC, :], ALU.subtract)
                nc.vector.tensor_tensor(M.cv_lo[:, :, 0:DC], cV[:], M.cv_hi[:, :, 0:DC], ALU.subtract)
                nc.vector.tensor_copy(M.C[0][0:DC, 1:17, 0:8], wv0[:])
                dve.wait_ge(tanh_done, 1)
                na = 0
                for g, (n, h, kind) in enumerate(groups):
                    L = LAYERS[n]
                    dve.wait_ge(prod, g + 1)
                    if kind == "A":
                        na += 1
                        dve.wait_ge(a_hi, na)
                        nc.vector.scalar_tensor_tensor(
                            M.A_lo[n][:, h:h + 4, :], M.ps[:, g % 6, 0:4 * DC].rearrange("p (h w) -> p h w", h=4),
                            QS * L.scale, M.A_hi[n][:, h:h + 4, :], ALU.mult, ALU.subtract).then_inc(evac, 1)
                    else:
                        nc.vector.tensor_scalar(
                            M.C[n][0:DC, h + 1:h + 5, 0:D], M.ps[0:DC, g % 6, :].rearrange("p (h w) -> p h w", h=4),
                            M.gate[0:DC, n:n + 1], None, ALU.mult).then_inc(evac, 1)
                    if g == after[0] - 1:
                        nc.vector.tensor_scalar(M.qbias[:], M.ps[0:DC, 6, 0:16], QS * L.scale, None, ALU.mult)
                        for m in range(4):
                            nc.vector.tensor_scalar(M.obias[:, m, :], M.ps[:, 7, m * D:(m + 1) * D],
                                                    M.gate[:, m:m + 1], None, ALU.mult)
                dve.wait_ge(loaded["ffn"], 5 * 16)
                for j in range(6):
                    w = IC[j % 3]
                    nc.vector.tensor_reduce(am[0:w, j:j + 1], wn[0:w, j, :], AX.X, ALU.max,
                                            apply_absolute_value=True)
                link(nc.vector.tensor_reduce(am[:, 6:7], wd[:], AX.X, ALU.max, apply_absolute_value=True))
                link(nc.vector.tensor_scalar(sc[:], am[:], 1.0 / QMAX, None, ALU.mult))
                nc.vector.tensor_copy(M.wgs[:], sc[:, 0:3])
                nc.vector.tensor_copy(M.wus[:], sc[:, 3:6])
                link(nc.vector.reciprocal(inv[:, 0:7], sc[:, 0:7]))
                for j in range(6):
                    w = IC[j % 3]
                    nc.vector.tensor_scalar(wr[0:w, j, :], wn[0:w, j, :], inv[0:w, j:j + 1], ROUND,
                                            ALU.mult, ALU.add)
                link(nc.vector.tensor_scalar(wdr[:], wd[:], inv[:, 6:7], ROUND, ALU.mult, ALU.add))
                for j in range(6):
                    w = IC[j % 3]
                    ins = nc.vector.tensor_scalar(wi[0:w, j, :], wr[0:w, j, :], ROUND, None, ALU.subtract)
                ins.then_inc(wq_ready, 1)
                link(nc.vector.tensor_scalar(wdr[:], wdr[:], ROUND, None, ALU.subtract))
                nc.vector.tensor_scalar(wdr[:], wdr[:], sc[:, 6:7], None, ALU.mult).then_inc(wq_ready, 1)
                dve.wait_ge(prod, len(groups) + 1)
                nc.vector.tensor_copy(M.wgq[:], M.ps[:, 0, 0:INTER])
                nc.vector.tensor_copy(M.wuq[:], M.ps[:, 1, 0:INTER])
                for c in range(3):
                    nc.vector.tensor_copy(M.wdT[0:IC[c], c, :], M.ps[0:IC[c], 2, c * P:(c + 1) * P])


def retire(nc, sems):
    for s in sems:
        nc.gpsimd.sem_clear(s)
        nc.release_semaphore(s)


def chained(eng, sem):
    count = [0]

    def link(ins):
        count[0] += 1
        ins.then_inc(sem, 1)
        eng.wait_ge(sem, count[0])

    return link


def layernorm(nc, M, k, split, plain, bias):
    s = M.sem_ln
    with ExitStack() as ctx:
        def sb(name, shape):
            return ctx.enter_context(nc.sbuf_tensor(f"ln{k}_{name}", shape, F32))

        st = sb("stats", [P, NT, 6])
        a, b, c, e = (sb(n, [P, NT]) for n in "abce")
        mean, ve, rstd = sb("mean", [P, NT]), sb("var_eps", [P, NT]), sb("rstd", [P, NT])
        stat0 = k * (NT + 5)
        splits0 = M.splits
        M.splits += split

        with nc.Block() as block:
            @block.vector
            def _(dve):
                for t in range(NT):
                    nc.vector.bn_stats(st[:, t, :], M.x[:, t, :]).then_inc(s["stat"], 1)
                dve.wait_ge(s["stat"], stat0 + NT)
                nc.vector.tensor_tensor(a[:], st[:, :, 1], st[:, :, 4], ALU.add).then_inc(s["stat"], 1)
                nc.vector.tensor_tensor(b[:], st[:, :, 1], st[:, :, 4], ALU.subtract).then_inc(s["stat"], 1)
                nc.vector.tensor_tensor(c[:], st[:, :, 2], st[:, :, 5], ALU.add).then_inc(s["stat"], 1)
                dve.wait_ge(s["stat"], stat0 + NT + 3)
                nc.vector.tensor_scalar(mean[:], a[:], 0.5, None, ALU.mult)
                nc.vector.tensor_tensor(e[:], b[:], b[:], ALU.mult).then_inc(s["stat"], 1)
                nc.vector.tensor_scalar(c[:], c[:], 1.0 / D, EPS, ALU.mult, ALU.add).then_inc(s["stat"], 1)
                dve.wait_ge(s["stat"], stat0 + NT + 5)
                nc.vector.scalar_tensor_tensor(ve[:], e[:], 0.25, c[:], ALU.mult, ALU.add).then_inc(s["var"], 1)
                dve.wait_ge(s["rstd"], k + 1)
                for t in range(NT):
                    nc.vector.tensor_scalar(M.xn[:, t, :], M.x[:, t, :], mean[:, t:t + 1], rstd[:, t:t + 1],
                                            ALU.subtract, ALU.mult).then_inc(s["norm"], 1)
                if split:
                    for q in range(NQ):
                        dve.wait_ge(s["hi"], splits0 * NQ + q + 1)
                        sl = slice(q * QB, (q + 1) * QB)
                        nc.vector.tensor_tensor(M.xt_lo[:, sl], M.ps[:, q, :], M.xt_hi[:, sl], ALU.subtract)

            @block.gpsimd
            def _(pool):
                pool.wait_ge(s["var"], k + 1)
                nc.gpsimd.tensor_tensor(rstd[:], ve[:], M.neghalf[:], ALU.pow).then_inc(s["rstd"], 1)
                if bias is not None:
                    pool.wait_ge(s["norm"], (k + 1) * NT)
                    nc.gpsimd.tensor_tensor(M.x[:], M.x[:],
                                            M.obias[:, bias:bias + 1, :].to_broadcast([P, NT, D]), ALU.add)

            @block.tensor
            def _(pe):
                for t in range(NT):
                    pe.wait_ge(s["norm"], k * NT + t + 1)
                    ins = nc.tensor.transpose(M.ps[:, t // TQ, (t % TQ) * P:(t % TQ + 1) * P], M.xn[:, t, :],
                                              M.ident[:])
                    if t % TQ == TQ - 1:
                        ins.then_inc(s["transposed"], 1)

            @block.scalar
            def _(act):
                for q in range(NQ):
                    act.wait_ge(s["transposed"], k * NQ + q + 1)
                    sl = slice(q * QB, (q + 1) * QB)
                    if plain:
                        nc.scalar.activation(M.xt[:, sl], M.ps[:, q, :], ACT.Copy)
                    if split:
                        nc.scalar.activation(M.xt_hi[:, sl], M.ps[:, q, :], ACT.Copy).then_inc(s["hi"], 1)


def attention(nc, M, layer):
    L = LAYERS[layer]
    H, wide = L.H, L.wide
    UQ = 8 if wide else 1
    MJ = 16 if wide else 2
    ST = (0, 2)
    UB = 4
    BANKS = (5, 6, 7)
    CW = L.CW
    ps, A_hi, A_lo, C = M.ps, M.A_hi[layer], M.A_lo[layer], M.C[layer]

    def pieces(qb, u):
        if wide:
            return [(2 * u + i, qb * QB, QB, i * QB, 2 * u + i == 0, 2 * u + i == NT - 1) for i in range(2)]
        return [(2 * (2 * qb + j) + i, (2 * qb + j) * SEQ, SEQ, j * QB + i * SEQ, i == 0, i == 1)
                for j in range(2) for i in range(2)]

    if wide:
        first_m = (0, 0, 2, 4, 7, 10, 13, 15)
        m = [[("m", k) for k in range(first_m[u], (*first_m, MJ)[u + 1])] for u in range(UQ)]
        tensor_ops = [[("st", 0), *m[u][:-2], ("av", 0), *m[u][-2:-1], ("av", 1), *m[u][-1:]] for u in range(UQ)]
        tensor_ops[0].insert(0, ("q", 0))
        tensor_ops[1][1:1] = [("r", 0), ("o", 0)]
        tensor_ops[2].insert(3, ("o", 1))
        in_order = [[op for op in ops if op[0] == "m"] for ops in tensor_ops]
        vector_ops = [[*ops[:-1], ("lo", 0), *ops[-1:]] for ops in in_order]
        vector_ops[0].insert(0, ("q", 0))
        vector_ops[1][:0] = [("d", 0), ("x", 0)]
        vector_ops[2][1:1] = [("d", 1), ("x", 1)]
        scalar_ops = [[("exp", 0)] for u in range(UQ)]
        scalar_ops[0].insert(0, ("q", 0))
        scalar_ops[1].append(("r", 0))
        scalar_ops[UQ - 1].append(("u", 0))
    else:
        tensor_ops = [[("q", 0), ("st", 0), ("m", 0), ("av", 0), ("o", 0), ("r", 0), ("av", 1), ("m", 1), ("o", 1)]]
        vector_ops = [[("q", 0), ("m", 0), ("d", 0), ("x", 0), ("lo", 0), ("m", 1), ("d", 1), ("x", 1)]]
        scalar_ops = [[("q", 0), ("exp", 0), ("r", 0), ("u", 0)]]

    def unit_ops(ops, qb, u, prep, last):
        out = []
        for kind, k in ops[u]:
            if kind in "qm" and not prep or kind == "r" and not prep and qb > 0:
                continue
            if kind in ("st", "exp", "lo") and last and qb == NQ - 1 and u == UQ - 1:
                continue
            out.append((kind, k))
        return out

    def bank_of(kind, k):
        if kind == "m":
            return 1 + (k + 1) % 2 if wide else 2
        return 1 if kind == "o" else 0

    in_bank = [[op for ops in tensor_ops for op in ops if op[0] in "mo" and bank_of(*op) == b] for b in range(3)]
    m_in_bank = [[op for op in ops if op[0] == "m"] for ops in in_bank]
    o_in_bank = [[op for op in ops if op[0] == "o"] for ops in in_bank]

    def job(h, qb, kind, k=0, prep=True):
        b = bank_of(kind, k)
        blk = qb if h is None else h * NQ + qb
        if b == 0:
            if h is None:
                return 0, 2 * blk + (kind == "r")
            return 0, 2 * NQ - 1 + 2 * blk + (kind == "r" and prep)
        if h is None:
            return b, blk * len(m_in_bank[b]) + m_in_bank[b].index((kind, k))
        before = NQ * len(m_in_bank[b])
        if prep:
            return b, before + blk * len(in_bank[b]) + in_bank[b].index((kind, k))
        return b, (before + (H - 1) * NQ * len(in_bank[b]) + qb * len(o_in_bank[b])
                   + o_in_bank[b].index((kind, k)))

    def row_of(hh, qb):
        return (1 - hh, qb - 1) if qb else (hh, NQ - 1)

    with ExitStack() as ctx:
        def sb(name, shape, dt):
            return ctx.enter_context(nc.sbuf_tensor(f"at{layer}_{name}", shape, dt))

        def sem(name):
            sems.append(nc.alloc_semaphore(f"at{layer}_{name}"))
            return sems[-1]

        sems = []

        q_hi = [sb(f"q_hi{i}", [DA, NTOK], F16) for i in range(2)]
        q_lo = [sb(f"q_lo{i}", [DC, NTOK], F16) for i in range(2)]
        p = [sb(f"p{i}", [P, 2 * QB], F32) for i in range(2)]
        p_hi = [sb(f"p_hi{i}", [P, 2 * QB], F16) for i in range(2)]
        p_lo = [sb(f"p_lo{i}", [P, 2 * QB], F16) for i in range(2)]
        nmax = sb("neg_max", [P, 2, TQ], F16)
        mpart = sb("max_part", [P, 16], F32)
        rden = sb("rden", [P, TQ], F32)
        qbias = sb("q_bias", [DC, 16], F32)

        st_ready = sem("scores_ready")
        exp_done = sem("exp_done")
        plo_done = sem("p_lo_done")
        av_done = sem("av_done")
        u_evac = sem("u_evac")
        job_ready = [sem(f"job_ready{b}") for b in range(3)]
        job_free = [sem(f"job_free{b}") for b in range(3)]
        qhi_done = sem("q_hi_done")
        nmax_done = sem("nmax_done")
        rden_done = sem("rden_done")
        waited = sem("waited")
        qbias_ready = sem("q_bias_ready")

        def each_head(eng, head):
            with eng.Fori(0, H // 2 - 1) as i:
                for hh in range(2):
                    head(i * 2 + hh, hh, True, False)
            head(H - 2, 0, True, False)
            head(H - 1, 1, False, True)

        o_sb = [sb(f"o{i}", [P, TQ, 8], F32) for i in range(2)] if layer == 0 else None
        o_stored = [sem(f"o_stored{i}") for i in range(2)]

        with nc.Block() as block:
            if layer == 0:
                @block.sync
                def _(sp):
                    def out(h, qb, at):
                        sp.wait_ge(job_free[at[0]], at[1] + 2)
                        tokens = slice((qb + NQ - 1) % NQ * QB, ((qb + NQ - 1) % NQ + 1) * QB)
                        sp.dma_start(M.o_dram[h if qb == 0 else h + 1, tokens, :].rearrange("(t p) d -> p t d", p=P),
                                     o_sb[qb % 2][:]).then_inc(o_stored[qb % 2], 16)

                    def head(h, hh, prep, last):
                        for qb in range(NQ):
                            out(h, qb, job(h, qb, "o", 1, prep))

                    each_head(sp, head)
                    out(H, 0, job(H - 1, NQ, "o", 1, False))
                    sp.wait_ge(o_stored[0], (2 * H + 1) * 16 + 16)
                    sp.wait_ge(o_stored[1], 2 * H * 16 + 16)

            @block.tensor
            def _(pe):
                def queries(h, buf, qb, at):
                    b, k = at
                    pe.wait_ge(job_free[b], k + 1)
                    sl, o = slice(qb * QB, (qb + 1) * QB), ps[0:DC, BANKS[b], :]
                    nc.tensor.matmul(o, A_hi[:, h, :], M.xt_hi[:, sl], start=True, stop=False)
                    nc.tensor.matmul(o, A_hi[:, h, :], M.xt_lo[:, sl], start=False, stop=False)
                    nc.tensor.matmul(o, A_lo[:, h, :], M.xt_hi[:, sl], start=False, stop=True
                                     ).then_inc(job_ready[b], 1)

                def maxscores(buf, qb, k, at, blk):
                    b, n = at
                    pe.wait_ge(job_free[b], n + 1)
                    if k == 0:
                        pe.wait_ge(qhi_done, blk + 1)
                    bank = BANKS[b]
                    if wide:
                        t, kb = divmod(k, NQ)
                        q0 = qb * QB + t * P
                        ins = nc.tensor.matmul(ps[:, bank, :], q_hi[buf][0:DC, q0:q0 + P],
                                               M.ct_hi[0:DC, kb * QB:(kb + 1) * QB], start=True, stop=True)
                    else:
                        k0 = (2 * qb + k) * SEQ
                        for t in range(2):
                            ins = nc.tensor.matmul(ps[:, bank, t * SEQ:(t + 1) * SEQ],
                                                   q_hi[buf][0:DC, k0 + t * P:k0 + (t + 1) * P],
                                                   M.ct_hi[0:DC, k0:k0 + SEQ], start=True, stop=True)
                    ins.then_inc(job_ready[b], 1)

                def maxrow(blk, par, at):
                    b, n = at
                    pe.wait_ge(nmax_done, blk + 1)
                    pe.wait_ge(job_free[b], n + 1)
                    for t in range(TQ):
                        ins = nc.tensor.matmul(ps[0:1, BANKS[b], t * P:(t + 1) * P], nmax[:, par, t:t + 1],
                                               M.ident16[:], start=True, stop=True)
                    ins.then_inc(job_ready[b], 1)

                def scores(buf, par, qb, u):
                    for c, q0, nq, at, _, _ in pieces(qb, u):
                        o = ps[:, ST[par] + at // QB, at % QB:at % QB + nq]
                        ks = slice(c * P, (c + 1) * P)
                        nc.tensor.matmul(o, M.ct_hi[:, ks], q_hi[buf][:, q0:q0 + nq], start=True, stop=False)
                        nc.tensor.matmul(o, M.ct_lo[:, ks], q_hi[buf][0:DC, q0:q0 + nq], start=False, stop=False)
                        ins = nc.tensor.matmul(o, M.ct_hi[0:DC, ks], q_lo[buf][:, q0:q0 + nq],
                                               start=False, stop=True)
                    ins.then_inc(st_ready, 1)

                def values(par, qb, u, half):
                    part = pieces(qb, u)
                    part = part[half * len(part) // 2:(half + 1) * len(part) // 2]
                    for c, q0, nq, at, first, last in part:
                        o = ps[:, UB, q0 - qb * QB:q0 - qb * QB + nq]
                        cols = slice(at, at + nq)
                        nc.tensor.matmul(o, M.cv_hi[:, c, :], p_hi[par][:, cols], start=first, stop=False)
                        nc.tensor.matmul(o, M.cv_lo[:, c, :], p_hi[par][:, cols], start=False, stop=False)
                        ins = nc.tensor.matmul(o, M.cv_hi[:, c, :], p_lo[par][:, cols], start=False, stop=last)
                    if half:
                        ins.then_inc(av_done, 1)

                def project(blk, upar, slot, half, at):
                    b, n = at
                    pe.wait_ge(job_free[b], n + 1)
                    if half == 0:
                        pe.wait_ge(u_evac, blk + 1)
                    for t in range(2):
                        ins = nc.tensor.matmul(ps[:, BANKS[b], t * (CW + 1):(t + 1) * (CW + 1)],
                                               M.U[:, upar, (2 * half + t) * P:(2 * half + t + 1) * P],
                                               C[:, slot, :], start=True, stop=True)
                    ins.then_inc(job_ready[b], 1)

                def head(h, hh, prep, last):
                    for qb in range(NQ):
                        blk = h * NQ + qb
                        for u in range(UQ):
                            n = blk * UQ + u
                            par = (qb * UQ + u) % 2
                            for kind, k in unit_ops(tensor_ops, qb, u, prep, last):
                                if kind == "q":
                                    queries(h + 1, 1 - hh, qb, job(h, qb, "q"))
                                elif kind == "m":
                                    maxscores(1 - hh, qb, k, job(h, qb, "m", k), (h + 1) * NQ + qb)
                                elif kind == "r":
                                    maxrow(blk + NQ - 1, (qb + 1) % 2, job(h, qb, "r", 0, prep))
                                elif kind == "o":
                                    project(blk, (qb + 1) % 2, h if qb == 0 else h + 1, k,
                                            job(h, qb, "o", k, prep))
                                elif kind == "st":
                                    pe.wait_ge(exp_done, 2 * n + 2)
                                    if last and (qb, u) == (NQ - 2, UQ - 1):
                                        pe.wait_ge(job_free[0], job(h, 0, "r", 0, False)[1] + 2)
                                    nu = (u + 1) % UQ
                                    nq = (qb + (nu == 0)) % NQ
                                    scores(1 - hh if nu == 0 and nq == 0 else hh, 1 - par, nq, nu)
                                elif kind == "av":
                                    if k == 0:
                                        pe.wait_ge(plo_done, n + 1)
                                    if k == 0 and u == 0:
                                        pe.wait_ge(u_evac, blk + 1)
                                    values(par, qb, u, k)

                for qb in range(NQ):
                    queries(0, 0, qb, job(None, qb, "q"))
                    for k in range(MJ):
                        maxscores(0, qb, k, job(None, qb, "m", k), qb)
                    if qb < NQ - 1:
                        maxrow(qb, qb % 2, job(None, qb, "r"))
                pe.wait_ge(job_free[0], job(None, NQ - 2, "r")[1] + 2)
                pe.wait_ge(job_free[0], job(None, NQ - 1, "q")[1] + 2)
                scores(0, 0, 0, 0)
                each_head(pe, head)
                for half in range(2):
                    project(H * NQ, 1, H, half, job(H - 1, NQ, "o", half, False))

            @block.scalar
            def _(act):
                act.sem_inc(exp_done, 2)

                def queries(h, buf, qb, at):
                    b, k = at
                    act.wait_ge(job_ready[b], k + 1)
                    o = q_hi[buf][0:DC, qb * QB:(qb + 1) * QB]
                    if layer == 0:
                        act.wait_ge(qbias_ready, 1)
                        act.sem_inc(waited, 1)
                        nc.scalar.activation(o, ps[0:DC, BANKS[b], :], ACT.Identity, bias=qbias[:, bass.ds(h, 1)]
                                             ).then_inc(qhi_done, 1)
                    else:
                        nc.scalar.activation(o, ps[0:DC, BANKS[b], :], ACT.Copy).then_inc(qhi_done, 1)

                def maxrow(buf, qb, at):
                    b, k = at
                    act.wait_ge(job_ready[b], k + 1)
                    nc.scalar.activation(q_hi[buf][DC:DA, qb * QB:(qb + 1) * QB], ps[0:1, BANKS[b], :], ACT.Copy
                                         ).then_inc(job_free[b], 1)

                def exps(n, par):
                    act.wait_ge(st_ready, n + 1)
                    act.wait_ge(av_done, n + 1)
                    s = ps[:, ST[par]:ST[par] + 2, :]
                    nc.scalar.activation(p[par][:].rearrange("p (b q) -> p b q", b=2), s, ACT.Exp,
                                         scale=1.0 / QS).then_inc(exp_done, 1)
                    nc.scalar.activation(p_hi[par][:].rearrange("p (b q) -> p b q", b=2), s, ACT.Exp,
                                         scale=1.0 / QS).then_inc(exp_done, 1)

                def head(h, hh, prep, last):
                    for qb in range(NQ):
                        blk = h * NQ + qb
                        for u in range(UQ):
                            n = blk * UQ + u
                            par = (qb * UQ + u) % 2
                            for kind, _ in unit_ops(scalar_ops, qb, u, prep, last):
                                if kind == "q":
                                    queries(h + 1, 1 - hh, qb, job(h, qb, "q"))
                                elif kind == "exp":
                                    exps(n + 1, 1 - par)
                                elif kind == "r":
                                    maxrow(*row_of(hh, qb), job(h, qb, "r", 0, prep))
                                elif kind == "u":
                                    act.wait_ge(av_done, n + 3)
                                    b, k = (job(h, qb - 1, "o", 1, prep) if qb or prep
                                            else job(h - 1, NQ - 1, "o", 1))
                                    act.wait_ge(job_ready[b], k + 1)
                                    nc.scalar.activation(M.U[:, qb % 2, :], ps[0:DA, UB, :], ACT.Copy
                                                         ).then_inc(u_evac, 1)

                for qb in range(NQ):
                    queries(0, 0, qb, job(None, qb, "q"))
                    if qb < NQ - 1:
                        maxrow(0, qb, job(None, qb, "r"))
                exps(0, 0)
                each_head(act, head)

            @block.gpsimd
            def _(pool):
                pool.sem_inc(av_done, 2)
                pool.sem_inc(u_evac, 1)
                for b in range(3):
                    pool.sem_inc(job_free[b], 1)
                pool.sem_inc(o_stored[0], 16)
                pool.sem_inc(o_stored[1], 16)
                if layer == 0:
                    nc.gpsimd.tensor_copy(qbias[:], M.qbias[:]).then_inc(qbias_ready, 1)

            @block.vector
            def _(dve):
                def queries(h, buf, qb, blk):
                    dve.wait_ge(qhi_done, blk + 1)
                    sl = slice(qb * QB, (qb + 1) * QB)
                    if layer == 0:
                        nc.vector.scalar_tensor_tensor(q_lo[buf][:, sl], ps[0:DC, BANKS[0], :],
                                                       M.qbias[:, bass.ds(h, 1)], q_hi[buf][0:DC, sl],
                                                       ALU.add, ALU.subtract).then_inc(job_free[0], 1)
                    else:
                        nc.vector.tensor_tensor(q_lo[buf][:, sl], ps[0:DC, BANKS[0], :], q_hi[buf][0:DC, sl],
                                                ALU.subtract).then_inc(job_free[0], 1)

                def maxscores(blk, par, k, at):
                    b, n = at
                    dve.wait_ge(job_ready[b], n + 1)
                    if wide:
                        nc.vector.tensor_reduce(mpart[:, k:k + 1], ps[:, BANKS[b], :], AX.X, ALU.max
                                                ).then_inc(job_free[b], 1)
                    else:
                        nc.vector.tensor_reduce(nmax[:, par, 2 * k:2 * k + 2],
                                                ps[:, BANKS[b], :].rearrange("p (t k) -> p t k", t=2),
                                                AX.X, ALU.max, negate=True).then_inc(job_free[b], 1)
                    if k == MJ - 1:
                        dve.wait_ge(job_free[b], n + 2)
                        if wide:
                            nc.vector.tensor_reduce(nmax[:, par, :], mpart[:].rearrange("p (t k) -> p t k", t=TQ), AX.X,
                                                    ALU.max, negate=True).then_inc(nmax_done, 1)
                        else:
                            dve.sem_inc(nmax_done, 1)

                def denominators(half, at):
                    dve.wait_ge(job_ready[at[0]], at[1] + 1)
                    v = ps[:, BANKS[at[0]], 0:2 * (CW + 1)].rearrange("p (t w) -> p t w", t=2)
                    nc.vector.reciprocal(rden[:, 2 * half:2 * half + 2].unsqueeze(2), v[:, :, CW:CW + 1]
                                         ).then_inc(rden_done, 1)

                def project(blk, qb, half, at, slot, before):
                    v = ps[:, BANKS[at[0]], 0:2 * (CW + 1)].rearrange("p (t w) -> p t w", t=2)
                    dve.wait_ge(rden_done, blk * 2 + half + 1)
                    if layer == 0 and half == 0:
                        dve.wait_ge(o_stored[(qb + 1) % 2], before * 16 + 16)
                    for t in range(2):
                        tile, r = qb * TQ + 2 * half + t, rden[:, 2 * half + t:2 * half + t + 1]
                        if layer == 0:
                            ins = nc.vector.scalar_tensor_tensor(
                                o_sb[(qb + 1) % 2][:, 2 * half + t, :], v[:, t, 0:CW], r,
                                M.vbias[:, slot, :], ALU.mult, ALU.add)
                        else:
                            ins = nc.vector.scalar_tensor_tensor(M.x[:, tile, :], v[:, t, 0:CW], r,
                                                                 M.x[:, tile, :], ALU.mult, ALU.add)
                    ins.then_inc(job_free[at[0]], 1)

                def lows(n, par):
                    dve.wait_ge(exp_done, 2 * n + 4)
                    nc.vector.tensor_tensor(p_lo[par][:], p[par][:], p_hi[par][:], ALU.subtract
                                            ).then_inc(plo_done, 1)

                def head(h, hh, prep, last):
                    for qb in range(NQ):
                        blk = h * NQ + qb
                        for u in range(UQ):
                            n = blk * UQ + u
                            par = (qb * UQ + u) % 2
                            for kind, k in unit_ops(vector_ops, qb, u, prep, last):
                                if kind == "q":
                                    queries(h + 1, 1 - hh, qb, (h + 1) * NQ + qb)
                                elif kind == "m":
                                    maxscores((h + 1) * NQ + qb, qb % 2, k, job(h, qb, "m", k))
                                elif kind == "d":
                                    denominators(k, job(h, qb, "o", k, prep))
                                elif kind == "x":
                                    project(blk, (qb + NQ - 1) % NQ, k, job(h, qb, "o", k, prep),
                                            h if qb == 0 else h + 1, h * 2 + qb // 2)
                                elif kind == "lo":
                                    lows(n + 1, 1 - par)

                for qb in range(NQ):
                    queries(0, 0, qb, qb)
                    for k in range(MJ):
                        maxscores(qb, qb % 2, k, job(None, qb, "m", k))
                lows(0, 0)
                each_head(dve, head)
                for half in range(2):
                    at = job(H - 1, NQ, "o", half, False)
                    denominators(half, at)
                    project(H * NQ, NQ - 1, half, at, H, 2 * H)
        retire(nc, sems)


def gathered_projection(nc, M):
    gathered = [nc.alloc_semaphore(f"gp_gathered{q}") for q in range(NQ)]
    transposed, evac, y_ready = (nc.alloc_semaphore(f"gp_{k}") for k in ("transposed", "evacuated", "y_ready"))
    with nc.Block() as block:
        def gather(eng, tiles):
            for t in tiles:
                b, eight = t // 2, t % 2
                src = M.o_dram[1 + 8 * eight:9 + 8 * eight, b * SEQ:(b + 1) * SEQ, :]
                eng.dma_start(M.xn[:, t, :], src.rearrange("h (i r) d -> h i (r d)", r=16)
                              ).then_inc(gathered[t // TQ], 16)

        @block.sync
        def _(sp):
            gather(sp, range(0, NT, 2))

        @block.tensor
        def _(pe):
            for q in range(NQ):
                pe.wait_ge(gathered[q], TQ * 16)
                for t in range(q * TQ, (q + 1) * TQ):
                    ins = nc.tensor.transpose(M.ps[:, q, (t % TQ) * P:(t % TQ + 1) * P], M.xn[:, t, :], M.ident[:])
                ins.then_inc(transposed, 1)
            for q in range(NQ):
                pe.wait_ge(evac, q + 1)
                for t in range(q * TQ, (q + 1) * TQ):
                    ins = nc.tensor.matmul(M.ps[:, 4 + q, (t % TQ) * D:(t % TQ + 1) * D],
                                           M.xt[:, t * P:(t + 1) * P], M.wo0[:], start=True, stop=True)
                ins.then_inc(y_ready, 1)

        @block.scalar
        def _(act):
            gather(act, range(1, NT, 2))
            for q in range(NQ):
                act.wait_ge(transposed, q + 1)
                nc.scalar.activation(M.xt[:, q * QB:(q + 1) * QB], M.ps[:, q, :], ACT.Copy).then_inc(evac, 1)

        @block.vector
        def _(dve):
            for q in range(NQ):
                dve.wait_ge(y_ready, q + 1)
                tiles = M.x[:, q * TQ:(q + 1) * TQ, :].rearrange("p t f -> p (t f)")
                nc.vector.scalar_tensor_tensor(tiles, M.ps[:, 4 + q, :], M.gate[:, 0:1], tiles, ALU.mult, ALU.add)
    retire(nc, [*gathered, transposed, evac, y_ready])


def quantised_ffn(nc, M):
    with ExitStack() as ctx:
        def sb(name, shape, dt=F32):
            return ctx.enter_context(nc.sbuf_tensor(f"qf_{name}", shape, dt))

        def sem(name):
            sems.append(nc.alloc_semaphore(f"qf_{name}"))
            return sems[-1]

        sems = []

        xq = sb("x_int", [P, NTOK], BF16)
        tmp = sb("tmp", [P, NTOK])
        h = sb("hidden", [P, 3, NTOK])
        gated = [sb(f"gated{i}", [P, QB]) for i in range(2)]
        sig = sb("sigmoid", [P, 2])
        mx, mall, sx, inv = sb("max", [P, 1]), sb("max_all", [P, 1]), sb("scale_x", [P, 1]), sb("inv_x", [P, 1])
        hm, hall, sh, invh = sb("hmax", [P, 3]), sb("hmax_all", [P, 3]), sb("scale_h", [P, 2]), sb("inv_h", [P, 1])
        gs, us, sd = sb("gate_scale", [P, 3]), sb("up_scale", [P, 3]), sb("down_scale", [P, 1])
        chain, sig_ready, exp_done = sem("chain"), sem("clip_ready"), sem("clip_exp")
        xmax, xmax_all, xq_done = sem("x_max"), sem("x_max_all"), sem("x_int_done")
        gate_ready, up_ready, silu_done, h_done = sem("gate_ready"), sem("up_ready"), sem("silu_done"), sem("h_done")
        hmax, hmax_all, hq_done, y_ready = sem("h_max"), sem("h_max_all"), sem("h_int_done"), sem("y_ready")
        jobs = [(q, c) for q in range(NQ) for c in range(3)]

        with nc.Block() as block:
            @block.scalar
            def _(act):
                nc.scalar.activation(sig[:], M.clip[:], ACT.Exp, scale=-1.0).then_inc(exp_done, 1)
                for k, (q, c) in enumerate(jobs):
                    w = IC[c]
                    act.wait_ge(gate_ready, k + 1)
                    if k >= 2:
                        act.wait_ge(h_done, k - 1)
                    nc.scalar.activation(gated[k % 2][0:w, :], M.ps[0:w, k % 4, :], ACT.Silu,
                                         scale=gs[0:w, c:c + 1]).then_inc(silu_done, 1)

            @block.gpsimd
            def _(pool):
                pool.wait_ge(xmax, 1)
                nc.gpsimd.partition_all_reduce(mall[:], mx[:], P, RMAX).then_inc(xmax_all, 1)
                pool.wait_ge(hmax, 1)
                nc.gpsimd.partition_all_reduce(hall[:], hm[:], P, RMAX).then_inc(hmax_all, 1)

            @block.vector
            def _(dve):
                link = chained(dve, chain)
                nc.vector.tensor_reduce(mx[:], M.xt[:], AX.X, ALU.max, apply_absolute_value=True
                                        ).then_inc(xmax, 1)
                nc.vector.memset(hm[:], 0.0)
                dve.wait_ge(exp_done, 1)
                link(nc.vector.tensor_scalar(sig[:], sig[:], 1.0, QMAX, ALU.add, ALU.mult))
                link(nc.vector.reciprocal(sig[:], sig[:]))
                dve.wait_ge(xmax_all, 1)
                link(nc.vector.tensor_tensor(sx[:], mall[:], sig[:, 0:1], ALU.mult))
                nc.vector.tensor_scalar(gs[:], M.wgs[:], sx[:, 0:1], None, ALU.mult)
                nc.vector.tensor_scalar(us[:], M.wus[:], sx[:, 0:1], None, ALU.mult)
                link(nc.vector.reciprocal(inv[:], sx[:]))
                link(nc.vector.tensor_scalar(tmp[:], M.xt[:], inv[:, 0:1], ROUND, ALU.mult, ALU.add))
                link(nc.vector.tensor_scalar(tmp[:], tmp[:], ROUND, QMAX, ALU.subtract, ALU.min))
                nc.vector.tensor_scalar(xq[:], tmp[:], -QMAX - 1.0, None, ALU.max).then_inc(xq_done, 1)
                for k, (q, c) in enumerate(jobs):
                    w = IC[c]
                    dve.wait_ge(silu_done, k + 1)
                    dve.wait_ge(up_ready, k + 1)
                    nc.vector.scalar_tensor_tensor(h[0:w, c, q * QB:(q + 1) * QB], M.ps[0:w, 4 + k % 4, :],
                                                   us[0:w, c:c + 1], gated[k % 2][0:w, :], ALU.mult, ALU.mult
                                                   ).then_inc(h_done, 1)
                dve.wait_ge(h_done, len(jobs))
                for c in range(3):
                    ins = nc.vector.tensor_reduce(hm[0:IC[c], c:c + 1], h[0:IC[c], c, :], AX.X, ALU.max,
                                                  apply_absolute_value=True)
                ins.then_inc(hmax, 1)
                dve.wait_ge(hmax_all, 1)
                link(nc.vector.tensor_reduce(sd[:], hall[:], AX.X, ALU.max))
                link(nc.vector.tensor_tensor(sh[:, 0:1], sd[:], sig[:, 1:2], ALU.mult))
                nc.vector.tensor_tensor(sh[:, 1:2], sh[:, 0:1], M.gate[:, 4:5], ALU.mult)
                link(nc.vector.reciprocal(invh[:], sh[:, 0:1]))
                for c in range(3):
                    w = IC[c]
                    link(nc.vector.tensor_scalar(h[0:w, c, :], h[0:w, c, :], invh[0:w, 0:1], ROUND,
                                                 ALU.mult, ALU.add))
                    link(nc.vector.tensor_scalar(h[0:w, c, :], h[0:w, c, :], ROUND, QMAX, ALU.subtract, ALU.min))
                    nc.vector.tensor_scalar(h[0:w, c, :], h[0:w, c, :], -QMAX - 1.0, None, ALU.max
                                            ).then_inc(hq_done, 1)
                for q in range(NQ):
                    dve.wait_ge(y_ready, q + 1)
                    tiles = M.x[:, q * TQ:(q + 1) * TQ, :].rearrange("p t f -> p (t f)")
                    nc.vector.scalar_tensor_tensor(tiles, M.ps[:, q, :], sh[:, 1:2], tiles, ALU.mult, ALU.add)

            @block.tensor
            def _(pe):
                pe.wait_ge(xq_done, 1)
                for k, (q, c) in enumerate(jobs):
                    w, sl = IC[c], slice(q * QB, (q + 1) * QB)
                    if k >= 4:
                        pe.wait_ge(h_done, k - 3)
                    nc.tensor.matmul(M.ps[0:w, k % 4, :], M.wgq[:, c * P:c * P + w], xq[:, sl],
                                     start=True, stop=True).then_inc(gate_ready, 1)
                    nc.tensor.matmul(M.ps[0:w, 4 + k % 4, :], M.wuq[:, c * P:c * P + w], xq[:, sl],
                                     start=True, stop=True).then_inc(up_ready, 1)
                pe.wait_ge(hq_done, 3)
                for t in range(NT):
                    for c in range(3):
                        w = IC[c]
                        ins = nc.tensor.matmul(M.ps[:, t // TQ, (t % TQ) * D:(t % TQ + 1) * D],
                                               h[0:w, c, t * P:(t + 1) * P], M.wdT[0:w, c, :],
                                               start=c == 0, stop=c == 2)
                    if t % TQ == TQ - 1:
                        ins.then_inc(y_ready, 1)
        retire(nc, sems)


def router(nc, M, d, layer):
    E = (0, 8, 8, 16)[layer]
    with ExitStack() as ctx:
        def sb(name, shape, dt=F32):
            return ctx.enter_context(nc.sbuf_tensor(f"rt{layer}_{name}", shape, dt))

        def sem(name):
            return nc.alloc_semaphore(f"rt{layer}_{name}")

        w = sb("w", [P, E])
        bias = sb("bias", [P, 1, E])
        b2 = sb("b2", [8, D])
        combT = sb("combT", [8, NTOK])
        iota = sb("iota", [P, 1, E])
        v, e, o1, o2, t = (sb(n, [P, NT, E]) for n in ("v", "e", "first", "second", "t"))
        m, m2, i, s, r = (sb(n, [P, NT, 1]) for n in ("m", "m2", "i", "s", "r"))
        loaded, iota_done, logits, chain = sem("loaded"), sem("iota"), sem("logits"), sem("chain")
        shifted, exp_done, comb_done = sem("shifted"), sem("exp"), sem("comb")
        combT_ready, combT_done, b2_ready = sem("combT_ready"), sem("combT_done"), sem("b2_ready")
        nload = {1: 2, 2: 3, 3: 1}[layer]

        def wide(ap):
            return ap.to_broadcast([P, NT, E])

        with nc.Block() as block:
            @block.sync
            def _(sp):
                sp.dma_start(w[:], d[f"L{layer}_router"]).then_inc(loaded, 16)
                if layer < 3:
                    sp.dma_start(bias[:, 0, :], d[f"L{layer}_router_b"]).then_inc(loaded, 16)
                if layer == 2:
                    sp.dma_start(b2[:], d["L2_b2"]).then_inc(loaded, 16)

            @block.gpsimd
            def _(pool):
                for k in range(E):
                    ins = nc.gpsimd.memset(iota[:, :, k:k + 1], float(k - E))
                ins.then_inc(iota_done, 1)

            @block.tensor
            def _(pe):
                pe.wait_ge(loaded, 16 * nload)
                for n in range(NT):
                    ins = nc.tensor.matmul(M.ps[:, 0, n * E:(n + 1) * E], M.xt[:, n * P:(n + 1) * P], w[:],
                                           start=True, stop=True)
                ins.then_inc(logits, 1)
                if layer == 2:
                    pe.wait_ge(comb_done, 1)
                    for n in range(NT):
                        ins = nc.tensor.transpose(M.ps[0:8, 4 + n // TQ, (n % TQ) * P:(n % TQ + 1) * P],
                                                  M.comb[:, n, 0:8], M.ident[:])
                    ins.then_inc(combT_ready, 1)
                    pe.wait_ge(combT_done, 1)
                    for n in range(NT):
                        ins = nc.tensor.matmul(M.ps[:, n // TQ, (n % TQ) * D:(n % TQ + 1) * D],
                                               combT[:, n * P:(n + 1) * P], b2[:], start=True, stop=True)
                    ins.then_inc(b2_ready, 1)

            @block.scalar
            def _(act):
                act.wait_ge(shifted, 1)
                if layer == 2:
                    nc.scalar.activation(s[:], r[:], ACT.Exp).then_inc(exp_done, 1)
                    act.wait_ge(combT_ready, 1)
                    nc.scalar.activation(combT[:].rearrange("e (b t) -> e b t", b=4), M.ps[0:8, 4:8, :], ACT.Copy
                                         ).then_inc(combT_done, 1)
                else:
                    nc.scalar.activation(e[:], e[:], ACT.Exp).then_inc(exp_done, 1)

            @block.vector
            def _(dve):
                link = chained(dve, chain)
                V = nc.vector

                def first_largest(values, top, onehot):
                    link(V.tensor_reduce(top[:], values[:], AX.X, ALU.max))
                    link(V.tensor_tensor(t[:], values[:], wide(top[:]), ALU.is_ge))
                    link(V.tensor_tensor(t[:], t[:], iota[:].to_broadcast([P, NT, E]), ALU.mult))
                    link(V.tensor_reduce(i[:], t[:], AX.X, ALU.min))
                    link(V.tensor_tensor(onehot[:], iota[:].to_broadcast([P, NT, E]), wide(i[:]), ALU.is_equal))

                dve.wait_ge(iota_done, 1)
                dve.wait_ge(logits, 1)
                lg = M.ps[:, 0, 0:NT * E].rearrange("p (n e) -> p n e", n=NT)
                if layer < 3:
                    link(V.tensor_tensor(v[:], lg, bias[:].to_broadcast([P, NT, E]), ALU.add))
                else:
                    link(V.tensor_copy(v[:], lg))
                gate = M.gate[:, 4 + layer:5 + layer]
                if layer != 2:
                    link(V.tensor_reduce(m[:], v[:], AX.X, ALU.max))
                    V.tensor_tensor(e[:], v[:], wide(m[:]), ALU.subtract).then_inc(shifted, 1)
                if layer == 1:
                    first_largest(v, m2, o1)
                    dve.wait_ge(exp_done, 1)
                    link(V.tensor_reduce(s[:], e[:], AX.X, ALU.add))
                    link(V.reciprocal(r[:], s[:]))
                    link(V.tensor_scalar(r[:], r[:], gate, None, ALU.mult))
                    V.tensor_tensor(M.comb[:, :, 0:E], o1[:], wide(r[:]), ALU.mult)
                if layer == 2:
                    first_largest(v, m, o1)
                    link(V.tensor_scalar(e[:], o1[:], -3.0e38, None, ALU.mult))
                    link(V.tensor_tensor(t[:], o1[:], v[:], ALU.mult))
                    link(V.tensor_tensor(v[:], v[:], t[:], ALU.subtract))
                    link(V.tensor_tensor(v[:], v[:], e[:], ALU.add))
                    first_largest(v, m2, o2)
                    V.tensor_tensor(r[:], m2[:], m[:], ALU.subtract).then_inc(shifted, 1)
                    dve.wait_ge(exp_done, 1)
                    link(V.tensor_scalar(m[:], s[:], 1.0, None, ALU.add))
                    link(V.reciprocal(m[:], m[:]))
                    link(V.tensor_scalar(m[:], m[:], gate, None, ALU.mult))
                    link(V.tensor_tensor(m2[:], m[:], s[:], ALU.mult))
                    link(V.tensor_tensor(o1[:], o1[:], wide(m[:]), ALU.mult))
                    link(V.tensor_tensor(o2[:], o2[:], wide(m2[:]), ALU.mult))
                    V.tensor_tensor(M.comb[:, :, 0:E], o1[:], o2[:], ALU.add).then_inc(comb_done, 1)
                    dve.wait_ge(b2_ready, 1)
                    xs = M.x[:].rearrange("p (b t) f -> p b (t f)", b=4)
                    V.tensor_tensor(xs, xs, M.ps[:, 0:4, :], ALU.add)
                if layer == 3:
                    dve.wait_ge(exp_done, 1)
                    link(V.tensor_reduce(s[:], e[:], AX.X, ALU.add))
                    link(V.reciprocal(s[:], s[:]))
                    link(V.tensor_tensor(e[:], e[:], wide(s[:]), ALU.mult))
                    first_largest(e, m, o1)
                    link(V.scalar_tensor_tensor(v[:], o1[:], -2.0, e[:], ALU.mult, ALU.add))
                    first_largest(v, m2, o2)
                    link(V.tensor_tensor(o1[:], o1[:], o2[:], ALU.add))
                    link(V.tensor_tensor(o1[:], o1[:], e[:], ALU.mult))
                    V.tensor_scalar(M.comb[:, :, 0:E], o1[:], gate, None, ALU.mult)
                    link(V.memset(o2[:, :, 0:2], 1.0))
                    V.tensor_scalar(M.comb[:, :, E:E + 2], o2[:, :, 0:2], gate, None, ALU.mult)


def expert_ffn(nc, M, d, layer):
    E, FC, two, gated = {1: (8, 4, False, True), 2: (8, 4, False, False), 3: (9, 1, True, True)}[layer]
    W = FC * P * (2 if gated else 1)
    NA, NG, NY = (2, 4, 2) if not two else (2, 2, 2)
    if not gated:
        NA, NG = 4, 0
    YB = NA + NG
    YW = 2 if two else 1
    halves = FC > 1
    AHEAD = FC - 1 if halves else 1
    turn = [(0, f) for f in range(AHEAD, FC)] + [(1, f) for f in range(AHEAD)]
    NH = 2 if halves else NG
    ps = M.ps

    with ExitStack() as ctx:
        def sb(name, shape, dt=F32):
            return ctx.enter_context(nc.sbuf_tensor(f"ex{layer}_{name}", shape, dt))

        def sem(name):
            sems.append(nc.alloc_semaphore(f"ex{layer}_{name}"))
            return sems[-1]

        sems = []

        raw = [sb(f"w1_raw{i}", [P, W]) for i in range(2)]
        w_hi = [sb(f"w1_hi{i}", [P, W], F16) for i in range(2)]
        w_lo = [sb(f"w1_lo{i}", [P, W], F16) for i in range(2)]
        w2 = [sb(f"w2_{i}", [P, FC, D]) for i in range(2)]
        if halves:
            w2_hi = [sb(f"w2_hi{i}", [P, FC, D], F16) for i in range(2)]
            w2_lo = [sb(f"w2_lo{i}", [P, FC, D], F16) for i in range(2)]
            hid_hi = [sb(f"hidden_hi{i}", [P, FC, QB], F16) for i in range(2)]
            hid_lo = [sb(f"hidden_lo{i}", [P, FC, QB], F16) for i in range(2)]
            hid1 = [sb(f"hidden{i}", [P, QB]) for i in range(2)]
        else:
            hid = [sb(f"hidden{i}", [P, FC, QB]) for i in range(2)]
        act_out = [sb(f"silu{i}", [P, QB]) for i in range(2)]
        b1 = sb("b1", [P, 8 * FC])
        b1_loaded = sem("b1_loaded")
        waited = sem("waited")
        w1_loaded, w2_loaded = [sem(f"w1_loaded{i}") for i in range(2)], [sem(f"w2_loaded{i}") for i in range(2)]
        w1_hi_done = sem("w1_hi_done")
        w1_done = sem("w1_split")
        w2_hi_done, w2_done = sem("w2_hi_done"), sem("w2_split")
        a_ready, g_ready = sem("a_ready"), sem("g_ready")
        silu_done = sem("silu_done")
        hi_done = sem("hi_done")
        hid_done = sem("hid_done")
        mult_done = sem("mult_done") if halves else hid_done
        y_ready = sem("y_ready")
        half_done = sem("half_done")
        y_done = sem("y_done")

        def each_expert(eng, expert):
            n = (E - 1) // 2
            with eng.Fori(0, n) as i:
                for j in range(2):
                    expert(i * 2 + j, j, False, i)
            for e in range(2 * n, E):
                expert(e, e % 2, e == E - 1, e // 2)

        with nc.Block() as block:
            @block.sync
            def _(sp):
                if not gated:
                    sp.dma_start(b1[:], d["L2_b1"]).then_inc(b1_loaded, 16)

                def load(e, j, last, times):
                    sp.wait_ge(w1_done, e + 1)
                    sp.dma_start(raw[j][:], d[f"L{layer}_w1"][e]).then_inc(w1_loaded[j], 16)
                    if halves:
                        sp.wait_ge(w2_done, e + 1)
                    else:
                        sp.wait_ge(y_ready, e * NQ + NQ)
                    sp.dma_start(w2[j][:], d[f"L{layer}_w2"][e].rearrange("(f p) n -> p f n", p=P)
                                 ).then_inc(w2_loaded[j], 16)

                each_expert(sp, load)

            @block.gpsimd
            def _(pool):
                pool.sem_inc(w1_done, 2)
                pool.sem_inc(silu_done, NA)
                pool.sem_inc(hid_done, NH)
                if halves:
                    pool.sem_inc(w2_done, 2)
                    if gated:
                        pool.sem_inc(mult_done, NG)
                pool.sem_inc(y_ready, 2 * NQ)
                pool.sem_inc(y_done, 2)

                def split(e, j, last, times):
                    pool.wait_ge(w1_loaded[j], times * 16 + 16)
                    pool.wait_ge(y_ready, e * NQ + NQ)
                    nc.gpsimd.tensor_tensor(w_hi[j][:], raw[j][:], M.one[:].to_broadcast([P, W]), ALU.mult
                                            ).then_inc(w1_hi_done, 1)
                    pool.wait_ge(w1_hi_done, e + 1)
                    nc.gpsimd.tensor_tensor(w_lo[j][:], raw[j][:], w_hi[j][:], ALU.subtract).then_inc(w1_done, 1)
                    if halves:
                        pool.wait_ge(w2_loaded[j], times * 16 + 16)
                        flat = [w[j][:].rearrange("p f n -> p (f n)") for w in (w2, w2_hi, w2_lo)]
                        nc.gpsimd.tensor_tensor(flat[1], flat[0], M.one[:].to_broadcast([P, FC * D]), ALU.mult
                                                ).then_inc(w2_hi_done, 1)
                        pool.wait_ge(w2_hi_done, e + 1)
                        nc.gpsimd.tensor_tensor(flat[2], flat[0], flat[1], ALU.subtract).then_inc(w2_done, 1)

                each_expert(pool, split)

            def each_step(e, j, last):
                for q in range(NQ):
                    n = e * NQ + q
                    for dn, f in turn:
                        if dn == 0:
                            yield "chunk", (e, j, q, f, n, n * FC + f)
                        elif not (last and q == NQ - 1):
                            at = (e, j, q + 1) if q < NQ - 1 else (e + 1, 1 - j, 0)
                            yield "chunk", (*at, f, n + 1, (n + 1) * FC + f)
                    yield "result", (e, j, q, n)

            begin = [(0, 0, 0, f, 0, f) for f in range(AHEAD)]

            @block.tensor
            def _(pe):
                def chunk(e, j, q, f, n, k):
                    if q == 0 and f == 0:
                        pe.wait_ge(w1_done, e + 3)
                    sl = slice(q * QB, (q + 1) * QB)
                    kk = q * FC + f

                    def product(bank, at):
                        nc.tensor.matmul(ps[:, bank, :], w_hi[j][:, at:at + P], M.xt_hi[:, sl],
                                         start=True, stop=False)
                        nc.tensor.matmul(ps[:, bank, :], w_lo[j][:, at:at + P], M.xt_hi[:, sl],
                                         start=False, stop=False)
                        return nc.tensor.matmul(ps[:, bank, :], w_hi[j][:, at:at + P], M.xt_lo[:, sl],
                                                start=False, stop=True)

                    pe.wait_ge(silu_done, k + 1)
                    product(kk % NA, f * P).then_inc(a_ready, 1)
                    if gated:
                        pe.wait_ge(mult_done, k + 1)
                        product(NA + kk % NG, (FC + f) * P).then_inc(g_ready, 1)

                def result(e, j, q, n, times):
                    pe.wait_ge(y_done, n + 1)
                    pe.wait_ge(hid_done, (n + 1) * FC + NH)
                    if q == 0 and halves:
                        pe.wait_ge(w2_done, e + 3)
                    elif q == 0:
                        pe.wait_ge(w2_loaded[j], times * 16 + 16)
                    y, b = YB + (q % NY) * YW, q % 2
                    for t in range(TQ):
                        tok = slice(t * P, (t + 1) * P)
                        if two:
                            for r in range(2):
                                half = slice(64 * r, 64 * r + 64)
                                ins = nc.tensor.matmul(ps[:, y + r, t * D:(t + 1) * D], hid[b][half, 0, tok],
                                                       w2[j][half, 0, :], start=True, stop=True)
                        else:
                            o = ps[:, y, t * D:(t + 1) * D]
                            for f in range(FC):
                                nc.tensor.matmul(o, hid_hi[b][:, f, tok], w2_hi[j][:, f, :],
                                                 start=f == 0, stop=False)
                                nc.tensor.matmul(o, hid_hi[b][:, f, tok], w2_lo[j][:, f, :],
                                                 start=False, stop=False)
                                ins = nc.tensor.matmul(o, hid_lo[b][:, f, tok], w2_hi[j][:, f, :],
                                                       start=False, stop=f == FC - 1)
                    ins.then_inc(y_ready, 1)

                def expert(e, j, last, times):
                    for kind, at in each_step(e, j, last):
                        if kind == "chunk":
                            chunk(*at)
                        else:
                            result(*at, times)

                for at in begin:
                    chunk(*at)
                each_expert(pe, expert)

            @block.scalar
            def _(act):
                def high(e, j, q, f, n, k):
                    act.wait_ge(mult_done, k + 1 + NG)
                    if f == 0:
                        act.wait_ge(y_ready, n + 2 * NQ - 1)
                    nc.scalar.activation(hid_hi[q % 2][:, f, :], hid1[f % 2][:], ACT.Copy).then_inc(hi_done, 1)

                def chunk(e, j, q, f, n, k, before):
                    act.wait_ge(a_ready, k + 1)
                    a = ps[:, (q * FC + f) % NA, :]
                    if gated:
                        act.wait_ge(mult_done, k - 1 + NG)
                        nc.scalar.activation(act_out[(q * FC + f) % 2][:], a, ACT.Silu).then_inc(silu_done, 1)
                        if halves and before:
                            high(*before)
                    else:
                        if f == 0:
                            act.wait_ge(y_ready, n + 2 * NQ - 1)
                        act.wait_ge(hid_done, k + 1)
                        act.wait_ge(b1_loaded, 16)
                        act.sem_inc(waited, 1)
                        bias = b1[:, bass.ds(e * FC + f, 1)]
                        nc.scalar.activation(hid_hi[q % 2][:, f, :], a, ACT.Gelu, bias=bias)
                        nc.scalar.activation(hid1[f % 2][:], a, ACT.Gelu, bias=bias).then_inc(silu_done, 1)

                state = [None]

                def step_chunk(*at):
                    chunk(*at, state[0])
                    state[0] = at

                def expert(e, j, last, times):
                    state[0] = (e, j, 0, AHEAD - 1, e * NQ, e * NQ * FC + AHEAD - 1)
                    for kind, at in each_step(e, j, last):
                        if kind == "chunk":
                            step_chunk(*at)
                    if last and halves and gated:
                        high(*state[0])

                for at in begin:
                    step_chunk(*at)
                each_expert(act, expert)

            @block.vector
            def _(dve):
                def mult(e, j, q, f, n, k):
                    if halves:
                        dve.wait_ge(hid_done, k + 1)
                        o = hid1[f % 2][:]
                    else:
                        dve.wait_ge(y_ready, n + 2 * NQ - 1)
                        o = hid[q % 2][:, f, :]
                    dve.wait_ge(silu_done, k + 1 + NA)
                    dve.wait_ge(g_ready, k + 1)
                    kk = q * FC + f
                    nc.vector.tensor_tensor(o, ps[:, NA + kk % NG, :], act_out[kk % 2][:], ALU.mult
                                            ).then_inc(mult_done if halves else hid_done, 1)

                def low(e, j, q, f, n, k):
                    if gated:
                        dve.wait_ge(hi_done, k + 1)
                    else:
                        dve.wait_ge(silu_done, k + 1 + NA)
                    nc.vector.tensor_tensor(hid_lo[q % 2][:, f, :], hid1[f % 2][:], hid_hi[q % 2][:, f, :],
                                            ALU.subtract).then_inc(hid_done, 1)

                def result(e, j, q, n):
                    dve.wait_ge(y_ready, n + 1 + 2 * NQ)
                    y = YB + (q % NY) * YW
                    for r in range(YW):
                        for t in range(TQ):
                            tile = q * TQ + t
                            ins = nc.vector.scalar_tensor_tensor(
                                M.x[:, tile, :], ps[:, y + r, t * D:(t + 1) * D],
                                M.comb[:, tile, bass.ds(e * YW + r, 1)], M.x[:, tile, :], ALU.mult, ALU.add)
                            if r == 0 and two:
                                ins.then_inc(half_done, 1)
                        if r == 0 and two:
                            dve.wait_ge(half_done, (n + 1) * TQ)
                    ins.then_inc(y_done, 1)

                def chunk(at, before):
                    if gated:
                        mult(*at)
                    if not gated:
                        low(*at)
                    elif halves and before:
                        low(*before)

                def expert(e, j, last, times):
                    before = (e, j, 0, AHEAD - 1, e * NQ, e * NQ * FC + AHEAD - 1)
                    for kind, at in each_step(e, j, last):
                        if kind == "chunk":
                            chunk(at, before)
                            before = at
                        else:
                            if last and at[2] == NQ - 1 and halves and gated:
                                low(*before)
                            result(*at)

                before = None
                for at in begin:
                    chunk(at, before)
                    before = at
                each_expert(dve, expert)
        retire(nc, sems)


def store(nc, M, out):
    stored = nc.alloc_semaphore("stored")
    with nc.Block() as block:
        @block.sync
        def _(sp):
            sp.dma_start(out.rearrange("b (t p) f -> p (b t) f", p=P), M.x[:]).then_inc(stored, 16)
            sp.wait_ge(stored, 16)


def kernel(**inputs):
    import concourse.bacc as bacc
    from concourse.bass_utils import run_bass_kernel_spmd

    a = {k: np.asarray(v) for k, v in inputs.items()}
    heads = lambda w, n, h: w.reshape(n, h, -1).transpose(1, 0, 2)
    dims = [(L.H, L.DH) for L in LAYERS]
    lay = {
        "x": a["x"].reshape(NTOK, D),
        "ctx": a["ctx_768"].reshape(NTOK, DC),
        "ctxT": a["ctx_768"].reshape(NTOK, DC).T,
        "g": np.broadcast_to(np.concatenate([a["g_xattn"], a["g_ffn"]]), (P, 8)),
        "clip": np.broadcast_to(np.concatenate([a["L0_ffn_clip_x"], a["L0_ffn_clip_down"]]), (P, 2)),
        "L0_q": heads(a["L0_xattn_q_w"], *dims[0]), "L0_k": heads(a["L0_xattn_v_w"], *dims[0]),
        "L0_wv": a["L0_xattn_v_w"].T.reshape(DC, 16, 8), "L0_wo": a["L0_xattn_o_w"].T,
        "L0_bq": a["L0_xattn_q_b"].reshape(16, 8).T,
        "L0_bv": np.broadcast_to(a["L0_xattn_v_b"].reshape(1, 16, 8), (P, 16, 8)),
        "bo": np.stack([a["L0_xattn_o_b"], a["L1_xattn_bo"], a["L2_xattn_bout"], a["L3_xattn_b_out"]])[None],
        "L0_gate": a["L0_ffn_w_gate"], "L0_up": a["L0_ffn_w_up"], "L0_down": a["L0_ffn_w_down"],
        "L1_q": heads(a["L1_xattn_Wq"].T, *dims[1]), "L1_k": heads(a["L1_xattn_Wk"].T, *dims[1]),
        "L1_v": heads(a["L1_xattn_Wv"].T, *dims[1]), "L1_o": heads(a["L1_xattn_Wo"], *dims[1]),
        "L1_router": a["L1_ffn_router_w"], "L1_router_b": np.broadcast_to(a["L1_ffn_router_b"], (P, 8)),
        "L1_w1": a["L1_ffn_w1"], "L1_w2": a["L1_ffn_w2"],
        "L2_q": heads(a["L2_xattn_Wq"].T, *dims[2]), "L2_k": heads(a["L2_xattn_Wk"].T, *dims[2]),
        "L2_v": heads(a["L2_xattn_Wv"].T, *dims[2]), "L2_o": heads(a["L2_xattn_Wout"], *dims[2]),
        "L2_router": a["L2_ffn_gate_w"], "L2_router_b": np.broadcast_to(a["L2_ffn_gate_b"], (P, 8)),
        "L2_w1": a["L2_ffn_w1"], "L2_w2": a["L2_ffn_w2"], "L2_b2": a["L2_ffn_b2"],
        "L2_b1": a["L2_ffn_b1"].reshape(8 * 4, P).T,
        "L3_q": heads(a["L3_xattn_w_q"].T, *dims[3]),
        "L3_k": heads(a["L3_xattn_w_kv"][:, :1024].T, *dims[3]),
        "L3_v": heads(a["L3_xattn_w_kv"][:, 1024:].T, *dims[3]),
        "L3_o": heads(a["L3_xattn_w_out"], *dims[3]),
        "L3_router": a["L3_ffn_router_w"],
        "L3_w1": np.concatenate([
            np.concatenate([w.reshape(8, 2, D, 64).transpose(0, 2, 1, 3).reshape(8, D, P), s[None]])
            for w, s in ((a["L3_ffn_gate_w"], a["L3_ffn_shared_gate_w"]), (a["L3_ffn_up_w"], a["L3_ffn_shared_up_w"]))
        ], axis=2),
        "L3_w2": np.concatenate([a["L3_ffn_down_w"].reshape(8, P, D), a["L3_ffn_shared_down_w"][None]]),
    }
    lay = {k: np.ascontiguousarray(v) for k, v in lay.items()}
    nc = bacc.Bacc("TRN2", target_bir_lowering=False, num_devices=1)
    d = {k: nc.dram_tensor(f"in_{k}", v.shape, mybir.dt.from_np(v.dtype), kind="ExternalInput").ap()
         for k, v in lay.items()}
    out = nc.dram_tensor("out", a["x"].shape, F32, kind="ExternalOutput").ap()
    build(nc, d, out)
    r = run_bass_kernel_spmd(nc, [{f"in_{k}": v for k, v in lay.items()}], core_ids=[0])
    return r.results[0]["out"]
```
